# Optimizing a Trainium2 kernel written in Bass

```python
import numpy as np
import jax
import jax.numpy as jnp

def _softmax(x, axis=-1):
    return jax.nn.softmax(x, axis=axis)

def _gelu(x):
    return jax.nn.gelu(x, approximate=True)

def _silu(x):
    return jax.nn.silu(x)

def _sigmoid(x):
    return jax.nn.sigmoid(x)

def _layernorm(x, axis=-1, eps=1e-05):
    m = jnp.mean(x, axis=axis, keepdims=True)
    v = jnp.var(x, axis=axis, keepdims=True)
    return (x - m) / jnp.sqrt(v + eps)

def _scatter_add(tgt, idx, src, axis=0):
    return tgt.at[idx].add(src)

def _segment_sum(src, seg, n):
    return jax.ops.segment_sum(src, seg, n)
kernel_name = 'mk_recurrent_d1_jaxref_r8_0f5f28'

def setup_inputs(seed: int=0):
    np.random.seed(seed)
    _w = jnp.asarray

    def _L0_attn_setup():
        import jax, jax.numpy as jnp
        import numpy as np
        D_MODEL = 512
        N_HEADS = 32
        HEAD_DIM = D_MODEL // N_HEADS
        CLIP_QKV = 8.0
        ALIBI_BIAS_MAX = 8.0
        LN_EPS = 1e-05

        def _alibi_slopes(n_heads: int, bias_max: float) -> jnp.ndarray:
            next_pow2 = 2 ** int(np.ceil(np.log2(n_heads)))
            m = np.arange(1, next_pow2 + 1, dtype=np.float32) * (bias_max / next_pow2)
            slopes = 1.0 / np.power(2.0, m)
            if next_pow2 != n_heads:
                slopes = np.concatenate([slopes[1::2], slopes[::2]])[:n_heads]
            return jnp.asarray(slopes)

        def _layer_norm(x, w, b):
            mu = jnp.mean(x, axis=-1, keepdims=True)
            var = jnp.mean(jnp.square(x - mu), axis=-1, keepdims=True)
            return (x - mu) * jax.lax.rsqrt(var + LN_EPS) * w + b
        key = jax.random.key(seed)
        ks = jax.random.split(key, 3)
        B, S = (1, 256)
        hidden_states = jax.random.normal(ks[0], (B, S, D_MODEL), dtype=jnp.float32)
        Wqkv = jax.random.normal(ks[1], (3 * D_MODEL, D_MODEL), dtype=jnp.float32) * 0.02
        Wout = jax.random.normal(ks[2], (D_MODEL, D_MODEL), dtype=jnp.float32) * 0.02
        return {'hidden_states': hidden_states, 'Wqkv': Wqkv, 'q_ln_w': jnp.ones((D_MODEL,), jnp.float32), 'q_ln_b': jnp.zeros((D_MODEL,), jnp.float32), 'k_ln_w': jnp.ones((D_MODEL,), jnp.float32), 'k_ln_b': jnp.zeros((D_MODEL,), jnp.float32), 'Wout': Wout}
    _L0_attn_in = _L0_attn_setup()

    def _L0_ffn_setup():
        import jax, jax.numpy as jnp
        import numpy as np
        GROUP_SIZE = 128

        def dequantize(imatrix, scales, zeros, group_size, out_dtype):
            rs = jnp.repeat(scales, group_size, axis=0)
            rz = jnp.repeat(zeros, group_size, axis=0)
            return ((imatrix.astype(rs.dtype) - rz.astype(rs.dtype)) * rs).astype(out_dtype)
        key = jax.random.key(seed)
        ks = jax.random.split(key, 10)
        H, I, G = (512, 1792, GROUP_SIZE)
        B, S = (4, 256)
        x = jax.random.normal(ks[0], (B, S, H), dtype=jnp.float32)
        gate_w = jax.random.randint(ks[1], (H, I), 0, 16, dtype=jnp.int32)
        gate_z = jax.random.randint(ks[2], (H // G, I), 0, 16, dtype=jnp.int32)
        gate_s = jax.random.uniform(ks[3], (H // G, I), dtype=jnp.float32) * 0.01
        up_w = jax.random.randint(ks[4], (H, I), 0, 16, dtype=jnp.int32)
        up_z = jax.random.randint(ks[5], (H // G, I), 0, 16, dtype=jnp.int32)
        up_s = jax.random.uniform(ks[6], (H // G, I), dtype=jnp.float32) * 0.01
        down_w = jax.random.randint(ks[7], (I, H), 0, 16, dtype=jnp.int32)
        down_z = jax.random.randint(ks[8], (I // G, H), 0, 16, dtype=jnp.int32)
        down_s = jax.random.uniform(ks[9], (I // G, H), dtype=jnp.float32) * 0.01
        return {'x': x, 'gate_w': gate_w, 'gate_z': gate_z, 'gate_s': gate_s, 'up_w': up_w, 'up_z': up_z, 'up_s': up_s, 'down_w': down_w, 'down_z': down_z, 'down_s': down_s}
    _L0_ffn_in = _L0_ffn_setup()
    _d = {'L0_attn_hidden_states': _L0_attn_in['hidden_states'], 'L0_attn_Wqkv': _L0_attn_in['Wqkv'], 'L0_attn_q_ln_w': _L0_attn_in['q_ln_w'], 'L0_attn_q_ln_b': _L0_attn_in['q_ln_b'], 'L0_attn_k_ln_w': _L0_attn_in['k_ln_w'], 'L0_attn_k_ln_b': _L0_attn_in['k_ln_b'], 'L0_attn_Wout': _L0_attn_in['Wout'], 'L0_ffn_gate_w': _L0_ffn_in['gate_w'], 'L0_ffn_gate_z': _L0_ffn_in['gate_z'], 'L0_ffn_gate_s': _L0_ffn_in['gate_s'], 'L0_ffn_up_w': _L0_ffn_in['up_w'], 'L0_ffn_up_z': _L0_ffn_in['up_z'], 'L0_ffn_up_s': _L0_ffn_in['up_s'], 'L0_ffn_down_w': _L0_ffn_in['down_w'], 'L0_ffn_down_z': _L0_ffn_in['down_z'], 'L0_ffn_down_s': _L0_ffn_in['down_s']}
    _x0 = _d['L0_attn_hidden_states']
    _d['L0_attn_hidden_states'] = jax.random.normal(jax.random.fold_in(jax.random.key(seed), 1), (2, 1024, 512), dtype=_x0.dtype)
    del _x0
    return _d

def reference(L0_attn_hidden_states, L0_attn_Wqkv, L0_attn_q_ln_w, L0_attn_q_ln_b, L0_attn_k_ln_w, L0_attn_k_ln_b, L0_attn_Wout, L0_ffn_gate_w, L0_ffn_gate_z, L0_ffn_gate_s, L0_ffn_up_w, L0_ffn_up_z, L0_ffn_up_s, L0_ffn_down_w, L0_ffn_down_z, L0_ffn_down_s):

    def _L0_attn_ref(hidden_states, Wqkv, q_ln_w, q_ln_b, k_ln_w, k_ln_b, Wout):
        import jax, jax.numpy as jnp
        import numpy as np
        D_MODEL = 512
        N_HEADS = 32
        HEAD_DIM = D_MODEL // N_HEADS
        CLIP_QKV = 8.0
        ALIBI_BIAS_MAX = 8.0
        LN_EPS = 1e-05

        def _alibi_slopes(n_heads: int, bias_max: float) -> jnp.ndarray:
            next_pow2 = 2 ** int(np.ceil(np.log2(n_heads)))
            m = np.arange(1, next_pow2 + 1, dtype=np.float32) * (bias_max / next_pow2)
            slopes = 1.0 / np.power(2.0, m)
            if next_pow2 != n_heads:
                slopes = np.concatenate([slopes[1::2], slopes[::2]])[:n_heads]
            return jnp.asarray(slopes)

        def _layer_norm(x, w, b):
            mu = jnp.mean(x, axis=-1, keepdims=True)
            var = jnp.mean(jnp.square(x - mu), axis=-1, keepdims=True)
            return (x - mu) * jax.lax.rsqrt(var + LN_EPS) * w + b
        B, S, _ = hidden_states.shape
        qkv = jnp.einsum('bsd,ed->bse', hidden_states, Wqkv)
        qkv = jnp.clip(qkv, -CLIP_QKV, CLIP_QKV)
        q, k, v = jnp.split(qkv, [D_MODEL, 2 * D_MODEL], axis=-1)
        q = _layer_norm(q, q_ln_w, q_ln_b)
        k = _layer_norm(k, k_ln_w, k_ln_b)
        q = q.reshape(B, S, N_HEADS, HEAD_DIM)
        k = k.reshape(B, S, N_HEADS, HEAD_DIM)
        v = v.reshape(B, S, N_HEADS, HEAD_DIM)
        scale = HEAD_DIM ** (-0.5)
        scores = jnp.einsum('bqhd,bkhd->bhqk', q, k) * scale
        slopes = _alibi_slopes(N_HEADS, ALIBI_BIAS_MAX)
        pos = jnp.arange(S)
        rel = (pos[None, :] - pos[:, None]).astype(jnp.float32)
        scores = scores + slopes[None, :, None, None] * rel[None, None]
        causal = pos[None, :] <= pos[:, None]
        scores = jnp.where(causal[None, None], scores, jnp.float32(-1e+30))
        probs = jax.nn.softmax(scores, axis=-1)
        out = jnp.einsum('bhqk,bkhd->bqhd', probs, v).reshape(B, S, D_MODEL)
        return jnp.einsum('bsd,ed->bse', out, Wout)

    def _L0_ffn_ref(x, gate_w, gate_z, gate_s, up_w, up_z, up_s, down_w, down_z, down_s):
        import jax, jax.numpy as jnp
        import numpy as np
        GROUP_SIZE = 128

        def dequantize(imatrix, scales, zeros, group_size, out_dtype):
            rs = jnp.repeat(scales, group_size, axis=0)
            rz = jnp.repeat(zeros, group_size, axis=0)
            return ((imatrix.astype(rs.dtype) - rz.astype(rs.dtype)) * rs).astype(out_dtype)
        dt = x.dtype
        gate_proj = dequantize(gate_w, gate_s, gate_z, GROUP_SIZE, dt)
        up_proj = dequantize(up_w, up_s, up_z, GROUP_SIZE, dt)
        down_proj = dequantize(down_w, down_s, down_z, GROUP_SIZE, dt)
        gate = jax.nn.silu(jnp.dot(x, gate_proj))
        up = jnp.dot(x, up_proj)
        return jnp.dot(gate * up, down_proj)
    x = L0_attn_hidden_states
    xn = _layernorm(x, axis=-1)
    s = _L0_attn_ref(xn, L0_attn_Wqkv, L0_attn_q_ln_w, L0_attn_q_ln_b, L0_attn_k_ln_w, L0_attn_k_ln_b, L0_attn_Wout)
    g = _silu(_L0_ffn_ref(xn, L0_ffn_gate_w, L0_ffn_gate_z, L0_ffn_gate_s, L0_ffn_up_w, L0_ffn_up_z, L0_ffn_up_s, L0_ffn_down_w, L0_ffn_down_z, L0_ffn_down_s))
    x = x + s * g
    return x

_drawn_inputs = setup_inputs


def setup_inputs(seed=0):
    import zlib

    import numpy as np

    out = dict(_drawn_inputs(seed))
    spreads = {'L0_attn_q_ln_w': (1.0, 0.6),
     'L0_attn_q_ln_b': (0.0, 0.8),
     'L0_attn_k_ln_w': (1.0, 0.6),
     'L0_attn_k_ln_b': (0.0, 0.8)}
    factors = {'L0_ffn_gate_s': 3.82, 'L0_ffn_up_s': 3.895, 'L0_ffn_down_s': 3.867}
    for name, (base, spread) in spreads.items():
        noise = np.random.default_rng([zlib.crc32(name.encode()), seed]).standard_normal(out[name].shape)
        drawn = base * np.exp(spread * noise) if base else spread * noise
        out[name] = jnp.asarray(drawn.astype(out[name].dtype))
    for name, factor in factors.items():
        out[name] = (out[name] * factor).astype(out[name].dtype)
    return out
```

```python
from contextlib import ExitStack

import concourse.bass as bass
from concourse import mybir

F32 = mybir.dt.float32
F32R = mybir.dt.float32r
BF16 = mybir.dt.bfloat16
I32 = mybir.dt.int32
ALU = mybir.AluOpType
ACT = mybir.ActivationFunctionType
AX = mybir.AxisListType

P = 128
BATCH, SEQ, D = 2, 1024, 512
HEADS, HD = 32, 16
INNER = 1792
TOK = BATCH * SEQ
TILES = TOK // P
KT = D // P
IT = INNER // P
GH = 4
GROUPS = HEADS // GH
NG = BATCH * GROUPS
QT = SEQ // P
VW = HD + 1
JOBS = 12
HALF = INNER // 2
NHALF = 2 * JOBS
CLIP = 8.0
EPS = 1e-5
SCALE = HD ** -0.5
ROWS_MAX = 108
ROWS = 111


def build(nc, x, wproj, lnw, w_all, z_all, s_all, ident_in, identb_in, tri_in, behind_in, qrows, krows, out):
    stk = nc.dram_tensor("stk", [2, NG, HD, 3, 2, GH, 512], BF16).ap()
    vscr = nc.dram_tensor("vscr", [BATCH, QT, P, GROUPS, GH * VW], F32).ap()

    x_t = x.rearrange("b (t p) d -> (b t) p d", p=P)
    out_t = out.rearrange("b (t p) d -> (b t) p d", p=P)

    with ExitStack() as ctx:
        def sem(name):
            return ctx.enter_context(nc.semaphore(name))

        def sb_in(c):
            return lambda name, shape, dt: c.enter_context(nc.sbuf_tensor(name, shape, dt))

        sb = sb_in(ctx)
        bank = [ctx.enter_context(nc.psum_tensor(f"bank{n}", [P, 512], F32)) for n in range(4)]
        pair = [ctx.enter_context(nc.psum_tensor(f"pair{n}", [P, 2, 512], F32)) for n in range(2)]

        w_f = sb("w_f", [P, JOBS * INNER], F32)
        wo_hi = sb("wo_hi", [P, KT, D], F32R)
        wo_lo = sb("wo_lo", [P, KT, D], F32R)
        ident = sb("ident", [P, P], F32)
        identb = sb("identb", [P, P], BF16)
        xmean = sb("xmean", [P, TILES], F32)
        xrstd = sb("xrstd", [P, TILES], F32)

        with ExitStack() as ca:
            sa = sb_in(ca)
            wq_hi = sa("wq_hi", [P, KT, 3 * D], F32R)
            wq_lo = sa("wq_lo", [P, KT, 3 * D], F32R)
            lnb = sa("lnb", [P, 4, D], F32)
            xin = sa("xin", [P, 2, D], F32)
            xn = sa("xn", [P, D], F32)
            xt_hi = sa("xt_hi", [P, 2, KT, P], F32R)
            xt_lo = sa("xt_lo", [P, 2, KT, P], F32R)
            qk = sa("qk", [P, 2, D], F32)
            res = sa("res", [P, 2, D], F32)
            parts = sa("parts", [P, 2, 3, KT, 2 * P], BF16)
            vst = sa("vst", [P, 2, HEADS, VW], F32)
            st6x = sa("st6x", [P, 6], F32)
            mvx = sa("mvx", [P, 2, 2], F32)
            st6q = sa("st6q", [P, 2, 6], F32)
            mvq = sa("mvq", [P, 2, 2], F32)
            vex = sa("vex", [P, 4], F32)
            rsq = sa("rsq", [P, 2], F32)
            mhalf = sa("mhalf", [P, 2], F32)

        o_sb = sb("o_sb", [P, NG, QT, GH * HD], F32)
        with ExitStack() as cb:
            sbb = sb_in(cb)
            qs = [sbb(f"qs{n}", [P, 2, GH, 512], BF16) for n in range(2)]
            ks = [sbb(f"ks{n}", [P, 2, GH, 512], BF16) for n in range(2)]
            vs = [sbb(f"vs{n}", [P, QT, GH * VW], F32) for n in range(2)]
            pr = [sbb(f"pr{n}", [P, GH, 512], F32) for n in range(3)]
            ot = sbb("ot", [P, 512], F32)
            tri = sbb("tri", [P, 512], F32)
            behind = sbb("behind", [P, P], BF16)
            zst = sbb("zst", [P, HALF], F32)
            sst = sbb("sst", [P, HALF], F32)
            mxa = sbb("mxa", [P, GH, 4], F32)
            mxb = sbb("mxb", [P, 2, GH, 4], F32)
            dneg = sbb("dneg", [P, 16], F32)
            dres = sbb("dres", [P, 16], F32)
            d3 = sbb("d3", [P, 3, 16], BF16)
            dt_sb = [sbb(f"dt{n}", [48, P], BF16) for n in range(2)]
            rec = sbb("rec", [P, 4, GH], F32)
        with ExitStack() as cc:
            sc = sb_in(cc)
            xc_hi = sc("xc_hi", [P, KT, 512], F32R)
            xc_lo = sc("xc_lo", [P, KT, 512], F32R)
            ws_hi = [sc(f"ws_hi{n}", [P, 3, 512], F32R) for n in range(2)]
            ws_lo = [sc(f"ws_lo{n}", [P, 3, 512], F32R) for n in range(2)]
            h_hi = [sc(f"h_hi{n}", [P, 512], F32R) for n in range(2)]
            h_lo = [sc(f"h_lo{n}", [P, 512], F32R) for n in range(2)]
            sg = [sc(f"sg{n}", [P, 512], F32) for n in range(2)]
            s_sb = sc("s_sb", [P, 4, 512], F32)
            xin_c = sc("xin_c", [P, 2, D], F32)
            ost = sc("ost", [P, 2, D], F32)
            oin = sc("oin", [P, D], F32)
            xnc = sc("xnc", [P, D], F32)

        def S(name):
            return sem(name)

        passed = {kind: S(f"passed_{kind}") for kind in ("pool", "dve", "pe")}

        def apart(eng, kind):
            eng.sem_inc(passed[kind], 1)

        raw_in, x_in = [S(f"raw_in{kt}") for kt in range(KT)], [S(f"x_in{u}") for u in range(2)]
        cst_in, w_in = S("cst_in"), S("w_in")
        setup_done = S("setup_done")
        whi_done, wlo_done = S("whi_done"), S("wlo_done")
        x_stat, x_mv, x_var, x_rstd, xn_done = S("x_stat"), S("x_mv"), S("x_var"), S("x_rstd"), S("xn_done")
        xt_ps, xhi_done, xlo_done = S("xt_ps"), S("xhi_done"), S("xlo_done")
        proj_v, proj_q, proj_k = S("proj_v"), S("proj_q"), S("proj_k")
        v_clip, v_out = S("v_clip"), [S(f"v_out{u}") for u in range(2)]
        qk_clip, qk_stat, qk_mv, qk_mid = S("qk_clip"), S("qk_stat"), S("qk_mv"), S("qk_mid")
        qk_var, qk_rstd, qk_ln = S("qk_var"), S("qk_rstd"), S("qk_ln")
        qk_ps, part_h, part_r, part_m, part_l, part_out = (
            S("qk_ps"), S("part_h"), S("part_r"), S("part_m"), S("part_l"), S("part_out"))

        LAST = TILES // 2 - 1
        b_xt, b_v, b_q, b_k = (bank[n] for n in range(4))
        b_t = [pair[0][:, n, :] for n in range(2)]

        def tile_pairs(eng, body):
            body(0, True, False)
            with eng.Fori(1, LAST) as c:
                body(c, False, False)
            body(LAST, False, True)

        with nc.Block() as block:
            @block.sync
            def _(sp):
                sp.dma_start(xin[:, 0, :], x_t[0]).then_inc(x_in[0], 16)
                for kt in range(KT):
                    sp.dma_start(w_f[:, kt * 2048:(kt + 1) * 2048], wproj[kt]).then_inc(raw_in[kt], 16)
                    if kt == 0:
                        sp.dma_start(ident[:, :], ident_in).then_inc(cst_in, 16)
                        sp.dma_start(identb[:, :], identb_in).then_inc(cst_in, 16)
                        sp.dma_start(xin[:, 1, :], x_t[1]).then_inc(x_in[1], 16)
                sp.dma_start(lnb[:, :, :], lnw.rearrange("(a n) d -> a n d", a=1).to_broadcast([P, 4, D]))\
                  .then_inc(cst_in, 16)

                def store_parts(c, need):
                    sp.wait_ge(part_l, need)
                    base = (c // 4) * GROUPS
                    half, tok = (c % 4) // 2, (c % 2) * 2 * P
                    for a in range(2):
                        for hh in range(2):
                            for j in range(GH):
                                p0 = hh * 64 + j * HD
                                for part in range(3):
                                    dst = stk[a, bass.ds(base, GROUPS), :, part, bass.ds(half, 1), j, bass.ds(tok, 2 * P)]
                                    dst = dst.rearrange("(ct h) c a s -> h c ct (a s)", h=2)[hh]
                                    sp.dma_start(dst, parts[p0:p0 + HD, a, part, :, :]).then_inc(part_out, 16)

                def body(c, first, last):
                    for u in range(2):
                        t = 2 * c + u
                        if not last:
                            sp.wait_ge(xn_done, t + 1)
                            sp.dma_start(xin[:, u, :], x_t[t + 2]).then_inc(x_in[u], 16)
                        sp.wait_ge(v_clip, t + 1)
                        sp.dma_start(vscr[t // QT, t % QT], vst[:, u, :, :].rearrange("p (g h) w -> p g (h w)", g=GROUPS))\
                          .then_inc(v_out[u], 16)
                        if u == 0 and not first:
                            store_parts(c - 1, 4 * c)
                    if first:
                        sp.wait_ge(wlo_done, KT)
                        for j in range(JOBS):
                            sp.dma_start(w_f[:, j * INNER:(j + 1) * INNER].bitcast(I32), w_all[j]).then_inc(w_in, 16)
                tile_pairs(sp, body)
                store_parts(LAST, 2 * TILES)
                sp.wait_ge(v_out[0], 8 * TILES)
                sp.wait_ge(v_out[1], 8 * TILES)
                sp.wait_ge(part_out, 16 * 48 * (LAST + 1))

            @block.gpsimd
            def _(pool):
                pool.memset(mhalf[:, :], -0.5).then_inc(setup_done, 1)
                pool.memset(vst[:, :, :, :], 1.0).then_inc(setup_done, 1)
                pool.wait_ge(setup_done, 2)

                def x_rs(t, u):
                    pool.wait_ge(x_mv, t + 1)
                    apart(pool, "pool")
                    pool.tensor_scalar(vex[:, 0:1], mvx[:, u, 1:2], EPS, None, ALU.add).then_inc(x_var, 1)
                    pool.wait_ge(x_var, t + 1)
                    apart(pool, "pool")
                    pool.tensor_tensor(xrstd[:, bass.ds(t, 1)], vex[:, 0:1], mhalf[:, 0:1], ALU.pow).then_inc(x_rstd, 1)

                def qk_rs(t):
                    pool.wait_ge(qk_mv, 2 * t + 2)
                    apart(pool, "pool")
                    pool.tensor_scalar(vex[:, 2:4], mvq[:, :, 1], EPS, None, ALU.add).then_inc(qk_var, 1)
                    pool.wait_ge(qk_var, t + 1)
                    pool.tensor_tensor(rsq[:, :], vex[:, 2:4], mhalf[:, :], ALU.pow).then_inc(qk_rstd, 1)

                def low(t, u):
                    for a in range(2):
                        pool.wait_ge(part_m, 2 * t + a + 1)
                        pool.tensor_tensor(parts[:, a, 2, :, u * P:(u + 1) * P],
                                           res[:, a, :].rearrange("p (k s) -> p k s", k=KT),
                                           parts[:, a, 1, :, u * P:(u + 1) * P], ALU.subtract).then_inc(part_l, 1)
                x_rs(0, 0)
                x_rs(1, 1)

                def body(c, first, last):
                    for u in range(2):
                        t = 2 * c + u
                        if not (first and u == 0):
                            qk_rs(t - 1)
                        if not last:
                            x_rs(t + 2, u)
                        if not (first and u == 0):
                            low(t - 1, 1 - u)
                tile_pairs(pool, body)
                qk_rs(TILES - 1)
                low(TILES - 1, 1)

            @block.scalar
            def _(act):
                for kt in range(KT):
                    act.wait_ge(raw_in[kt], 16)
                    raw = w_f[:, kt * 2048:(kt + 1) * 2048]
                    act.activation(wq_hi[:, kt, :], raw[:, 0:3 * D], ACT.Copy)
                    act.activation(wo_hi[:, kt, :], raw[:, 3 * D:], ACT.Copy).then_inc(whi_done, 1)

                def x_hi(t, u):
                    act.wait_ge(xt_ps, t + 1)
                    if not (isinstance(t, int) and t < 2):
                        act.wait_ge(proj_k, t - 1)
                    act.activation(xt_hi[:, u, :, :].rearrange("p k s -> p (k s)"), b_xt[:, :], ACT.Copy)\
                       .then_inc(xhi_done, 1)

                def high(t, u, a):
                    act.wait_ge(qk_ps, 2 * t + a + 1)
                    act.activation(parts[:, a, 0, :, u * P:(u + 1) * P],
                                   b_t[a].rearrange("p (k s) -> p k s", k=KT), ACT.Copy).then_inc(part_h, 1)

                def mid(t, u, a):
                    act.wait_ge(part_r, 2 * t + a + 1)
                    act.activation(parts[:, a, 1, :, u * P:(u + 1) * P],
                                   res[:, a, :].rearrange("p (k s) -> p k s", k=KT), ACT.Copy).then_inc(part_m, 1)

                def split(t, u, c_stored):
                    if c_stored is not None:
                        act.wait_ge(part_out, c_stored)
                    high(t, u, 0)
                    high(t, u, 1)
                    mid(t, u, 0)
                    mid(t, u, 1)
                x_hi(0, 0)

                def body(c, first, last):
                    for u in range(2):
                        t = 2 * c + u
                        if not (last and u == 1):
                            x_hi(t + 1, 1 - u)
                        if not (first and u == 0):
                            split(t - 1, 1 - u, None if first else 16 * 48 * c if u == 1 else None)
                tile_pairs(act, body)
                split(TILES - 1, 1, None)

            @block.vector
            def _(dve):
                def x_stats(t, u, c):
                    dve.wait_ge(x_in[u], 16 * c + 16)
                    dve.bn_stats(st6x[:, :], xin[:, u, :]).then_inc(x_stat, 1)
                    dve.wait_ge(x_stat, t + 1)
                    apart(dve, "dve")
                    dve.bn_aggr(mvx[:, u, :], st6x[:, :]).then_inc(x_mv, 1)
                    dve.wait_ge(x_mv, t + 1)
                    apart(dve, "dve")
                    dve.tensor_copy(xmean[:, bass.ds(t, 1)], mvx[:, u, 0:1])

                def x_norm(t, u):
                    dve.wait_ge(x_rstd, t + 1)
                    if not (isinstance(t, int) and t < 1):
                        dve.wait_ge(xt_ps, t)
                    dve.tensor_scalar(xn[:, :], xin[:, u, :], mvx[:, u, 0:1], xrstd[:, bass.ds(t, 1)],
                                      ALU.subtract, ALU.mult).then_inc(xn_done, 1)

                def x_lo(t, u):
                    dve.wait_ge(xhi_done, t + 1)
                    dve.tensor_tensor(xt_lo[:, u, :, :].rearrange("p k s -> p (k s)"), b_xt[:, :],
                                      xt_hi[:, u, :, :].rearrange("p k s -> p (k s)").bitcast(F32), ALU.subtract)\
                       .then_inc(xlo_done, 1)

                def clip_stats(t, a):
                    dve.wait_ge((proj_q, proj_k)[a], t + 1)
                    if not (isinstance(t, int) and t < 1):
                        dve.wait_ge(qk_ps, 2 * t - 1 + a)
                    dve.tensor_scalar(qk[:, a, :], (b_q, b_k)[a][:, :], CLIP, -CLIP, ALU.min, ALU.max).then_inc(qk_clip, 1)
                    dve.wait_ge(qk_clip, 2 * t + a + 1)
                    dve.bn_stats(st6q[:, a, :], qk[:, a, :]).then_inc(qk_stat, 1)
                    dve.wait_ge(qk_stat, 2 * t + a + 1)
                    apart(dve, "dve")
                    dve.bn_aggr(mvq[:, a, :], st6q[:, a, :]).then_inc(qk_mv, 1)

                def center(t, a):
                    dve.wait_ge(qk_mv, 2 * t + a + 1)
                    dve.scalar_tensor_tensor(out=qk[:, a, :], in0=qk[:, a, :], scalar=mvq[:, a, 0:1],
                                             in1=lnb[:, 2 * a, :], op0=ALU.subtract, op1=ALU.mult).then_inc(qk_mid, 1)

                def rescale(t, a):
                    dve.wait_ge(qk_mid, 2 * t + a + 1)
                    dve.wait_ge(qk_rstd, t + 1)
                    dve.scalar_tensor_tensor(out=qk[:, a, :], in0=qk[:, a, :], scalar=rsq[:, a:a + 1],
                                             in1=lnb[:, 2 * a + 1, :], op0=ALU.mult, op1=ALU.add).then_inc(qk_ln, 1)

                def residual(t, u, a):
                    dve.wait_ge(part_h, 2 * t + a + 1)
                    if not (isinstance(t, int) and t < 1):
                        dve.wait_ge(part_l, 2 * t - 1 + a)
                    dve.tensor_tensor(res[:, a, :].rearrange("p (k s) -> p k s", k=KT),
                                      b_t[a].rearrange("p (k s) -> p k s", k=KT),
                                      parts[:, a, 0, :, u * P:(u + 1) * P], ALU.subtract).then_inc(part_r, 1)

                x_stats(0, 0, 0)
                for kt in range(KT):
                    dve.wait_ge(whi_done, kt + 1)
                    raw = w_f[:, kt * 2048:(kt + 1) * 2048]
                    dve.tensor_tensor(wq_lo[:, kt, :], raw[:, 0:3 * D], wq_hi[:, kt, :].bitcast(F32), ALU.subtract)
                    dve.tensor_tensor(wo_lo[:, kt, :], raw[:, 3 * D:], wo_hi[:, kt, :].bitcast(F32), ALU.subtract)\
                       .then_inc(wlo_done, 1)
                    if kt == 0:
                        x_norm(0, 0)
                        x_stats(1, 1, 0)
                x_lo(0, 0)
                x_norm(1, 1)
                dve.wait_ge(setup_done, 2)
                dve.wait_ge(cst_in, 48)

                def body(c, first, last):
                    for u in range(2):
                        t = 2 * c + u
                        prev = not (first and u == 0)
                        if prev:
                            clip_stats(t - 1, 1)
                            center(t - 1, 0)
                            center(t - 1, 1)
                        if not last:
                            x_stats(t + 2, u, c + 1)
                        if prev:
                            rescale(t - 1, 0)
                            rescale(t - 1, 1)
                        dve.wait_ge(proj_v, t + 1)
                        if not first:
                            dve.wait_ge(v_out[u], 16 * c)
                        dve.tensor_scalar(vst[:, u, :, 0:HD], b_v[:, :].rearrange("p (h d) -> p h d", h=HEADS),
                                          CLIP, -CLIP, ALU.min, ALU.max).then_inc(v_clip, 1)
                        if not (last and u == 1):
                            x_lo(t + 1, 1 - u)
                        if not last:
                            x_norm(t + 2, u)
                        clip_stats(t, 0)
                        if prev:
                            residual(t - 1, 1 - u, 0)
                            residual(t - 1, 1 - u, 1)
                tile_pairs(dve, body)
                t = TILES - 1
                clip_stats(t, 1)
                for a in range(2):
                    center(t, a)
                for a in range(2):
                    rescale(t, a)
                for a in range(2):
                    residual(t, 1, a)

            @block.tensor
            def _(pe):
                def x_trans(t):
                    pe.wait_ge(xn_done, t + 1)
                    if not (isinstance(t, int) and t < 1):
                        pe.wait_ge(xlo_done, t)
                    for kt in range(KT):
                        mm = pe.transpose(b_xt[:, kt * P:(kt + 1) * P], xn[:, kt * P:(kt + 1) * P], ident[:, :])
                    mm.then_inc(xt_ps, 1)

                def project(t, u, n, b, done, free):
                    pe.wait_ge(xlo_done, t + 1)
                    if not (isinstance(t, int) and t < 1):
                        pe.wait_ge(*free)
                    cols = slice(n * D, (n + 1) * D)
                    for kt in range(KT):
                        if isinstance(t, int) and t < 1 and n == 2:
                            pe.wait_ge(wlo_done, kt + 1)
                        for i, (l, r) in enumerate(((xt_lo, wq_hi), (xt_hi, wq_lo), (xt_hi, wq_hi))):
                            mm = pe.matmul(b[:, :], l[:, u, kt, :], r[:, kt, cols],
                                           start=(kt == 0 and i == 0), stop=(kt == KT - 1 and i == 2))
                    mm.then_inc(done, 1)

                def qk_trans(t):
                    for a in range(2):
                        pe.wait_ge(qk_ln, 2 * t + a + 1)
                        if not (isinstance(t, int) and t < 1):
                            pe.wait_ge(part_r, 2 * t - 1 + a)
                        for kt in range(KT):
                            mm = pe.transpose(b_t[a][:, kt * P:(kt + 1) * P], qk[:, a, kt * P:(kt + 1) * P], ident[:, :])
                        mm.then_inc(qk_ps, 1)
                pe.wait_ge(cst_in, 48)
                x_trans(0)

                def body(c, first, last):
                    for u in range(2):
                        t = 2 * c + u
                        project(t, u, 2, b_v, proj_v, (v_clip, t))
                        if not (last and u == 1):
                            x_trans(t + 1)
                        project(t, u, 0, b_q, proj_q, (qk_clip, 2 * t - 1))
                        if not (first and u == 0):
                            qk_trans(t - 1)
                        project(t, u, 1, b_k, proj_k, (qk_clip, 2 * t))
                tile_pairs(pe, body)
                qk_trans(TILES - 1)

        mask_in = S("mask_in")
        tri_done, stk_in = S("tri_done"), [S(f"stk_in{n}") for n in range(2)]
        m_full, m_free = S("m_full"), S("m_free")
        s_full, s_free = [S(f"s_full{n}") for n in range(2)], [S(f"s_free{n}") for n in range(2)]
        exp_done, pv_done = S("exp_done"), S("pv_done")
        mxb_done, d_chain, d_copied, da_in, db_in = S("mxb_done"), S("d_chain"), S("d_copied"), S("da_in"), S("db_in")
        ot_done, rec_done, o_clear = S("ot_done"), S("rec_done"), S("o_clear")
        z_in, z_conv, z_sub, z_mul = S("z_in"), S("z_conv"), S("z_sub"), S("z_mul")

        b_m, b_o = bank[0:3], bank[3]
        STEPS = [(qb, kt, max(0, (kt - 4 * qb) * P)) for qb in range(2) for kt in range(4 * qb + 4)]
        NSTEP = len(STEPS)
        diag = [kt >= 4 * qb for qb, kt, _ in STEPS]

        def pieces(tiles):
            return [(qt, j, k0, min(512, (qt + 1) * P - k0))
                    for qt in tiles for j in range(GH) for k0 in range(0, (qt + 1) * P, 512)]
        LATE, EARLY = pieces([7]), pieces(range(7))
        NPC, PREP = len(LATE) + len(EARLY), len(EARLY)
        assert NPC % 3 == 0
        number = {pc: n for n, pc in enumerate(LATE + EARLY)}
        def n_slot(pc):
            return (PREP + number[pc]) % 3

        HELD = 3
        GAP = 5

        def spread(lot, lo, hi):
            width = [512 - STEPS[h // 2][2] for h in range(2 * NSTEP)]
            total, work = sum(width[lo:hi]), sum(pc[3] + 60 for pc in lot)
            plan, at, passed = {h: [] for h in range(lo, hi)}, 0, 0
            for h in range(lo, hi):
                passed += width[h]
                while at < len(lot) and (h == hi - 1 or sum(pc[3] + 60 for pc in lot[:at]) < work * passed / total):
                    plan[h].append(lot[at])
                    at += 1
            return plan
        plan = spread(LATE, 0, 6) | {6: [], 7: []} | spread(EARLY[GAP:-HELD], 8, 2 * NSTEP)
        last_a = max(number[pc] for pc in EARLY if pc[0] < 4)
        DA_AT = max(h for h, lot in plan.items() if any(pc[0] < 4 for pc in lot)) // 2 + 1
        O0_AT = 5
        USES = NSTEP + 2
        DB_USE, DA_USE, O0_USE, O1_USE = 4, DA_AT + 2, O0_AT + 1, USES - 1
        EXTRA = 1
        PV0 = 3

        EX = 2

        def use(e, p, last):
            return e + (e >= 4) + (e > DA_AT and not last) if p == 0 else e + (e > O0_AT)

        def full(i, n, p):
            return USES * i + n + (2 if p == 0 else 1)

        def groups(eng, body):
            with eng.Fori(0, NG // 2 - 1) as ip:
                for s in range(2):
                    body(2 * ip + s, s, ip, None)
            for s in range(2):
                body(NG - 2 + s, s, NG // 2 - 1, s == 1)

        with nc.Block() as block:
            @block.sync
            def _(sp):
                def load(i, s):
                    for a, dst in ((0, qs[s]), (1, ks[s])):
                        flat = dst[:, :, :, :].rearrange("p b j s -> p (b j s)")
                        src = stk[a, i].rearrange("c w b j s -> c w (b j s)")
                        for base, n, kpart in ((0, 3, 0), (48, 2, 1), (80, 1, 2)):
                            part = src[:, 0:n, :] if a == 0 else src[:, kpart:kpart + 1, :].to_broadcast([HD, n, GH * SEQ])
                            sp.dma_start(flat[base:base + n * HD, :], part).then_inc(stk_in[s], 16)
                    g = i % GROUPS
                    sp.dma_start(qs[s][96:ROWS_MAX, :, :, :].rearrange("p b j s -> p (b j s)"), qrows[g]).then_inc(stk_in[s], 16)
                    sp.dma_start(ks[s][96:ROWS, :, :, :].rearrange("p b j s -> p (b j s)"), krows[g]).then_inc(stk_in[s], 16)
                    sp.dma_start(vs[s][:, :, :], vscr[i // GROUPS, :, :, g, :].rearrange("t p w -> p t w"))\
                      .then_inc(stk_in[s], 16)

                def send_d(s, b, done, n):
                    sp.wait_ge(d_copied, n)
                    dst = qs[s][ROWS_MAX:ROWS, b, :, :].rearrange("a j (t c) -> a (j t) c", c=P)
                    sp.dma_start(dst, dt_sb[b][:, :]).then_inc(done, 16)

                def half_job(jj):
                    if not (isinstance(jj, int) and jj == 0):
                        sp.wait_ge(z_mul, jj)
                    sp.dma_start(zst[:, :].bitcast(I32), z_all[bass.ds(jj, 1), :].to_broadcast([P, HALF])).then_inc(z_in, 16)
                    sp.dma_start(sst[:, :], s_all[bass.ds(jj, 1), :].to_broadcast([P, HALF])).then_inc(z_in, 16)

                load(0, 0)
                sp.dma_start(tri[:, :], tri_in).then_inc(tri_done, 16)
                sp.dma_start(behind[:, :], behind_in).then_inc(mask_in, 16)
                load(1, 1)
                half_job(0)
                send_d(0, 0, da_in, 1)

                def body(i, s, ip, last):
                    send_d(s, 1, db_in, 2 * i + 2)
                    if not last:
                        half_job(3 * ip + (1, 3)[s])
                        send_d(1 - s, 0, da_in, 2 * i + 3)
                    if s == 0:
                        half_job(3 * ip + 2)
                    if last is None:
                        sp.wait_ge(pv_done, PV0 + NSTEP * i + NSTEP)
                        load(i + 2, s)
                groups(sp, body)

            @block.gpsimd
            def _(pool):
                pool.sem_inc(s_free[1], EXTRA)
                pool.sem_inc(ot_done, EXTRA)
                pool.sem_inc(pv_done, PV0)
                pool.sem_inc(exp_done, EX)

                def chain(mx, n):
                    apart(pool, "pool")
                    pool.tensor_scalar(dneg[:, :], mx.rearrange("p j t -> p (j t)"), -1.0, None, ALU.mult).then_inc(d_chain, 1)
                    pool.wait_ge(d_chain, 5 * n + 1)
                    apart(pool, "pool")
                    pool.tensor_copy(d3[:, 0, :], dneg[:, :]).then_inc(d_chain, 1)
                    pool.wait_ge(d_chain, 5 * n + 2)
                    pool.tensor_tensor(dres[:, :], dneg[:, :], d3[:, 0, :], ALU.subtract).then_inc(d_chain, 1)
                    pool.wait_ge(d_chain, 5 * n + 3)
                    apart(pool, "pool")
                    pool.tensor_copy(d3[:, 1, :], dres[:, :]).then_inc(d_chain, 1)
                    pool.wait_ge(d_chain, 5 * n + 4)
                    pool.tensor_tensor(d3[:, 2, :], dres[:, :], d3[:, 1, :], ALU.subtract).then_inc(d_chain, 1)

                def job(jj):
                    w = w_f[:, bass.ds(jj * HALF, HALF)]
                    pool.wait_ge(z_conv, jj + 1)
                    apart(pool, "pool")
                    pool.tensor_tensor(w, w, zst[:, :], ALU.subtract).then_inc(z_sub, 1)
                    pool.wait_ge(z_sub, jj + 1)
                    apart(pool, "pool")
                    pool.tensor_tensor(w, w, sst[:, :], ALU.mult).then_inc(z_mul, 1)

                pool.wait_ge(m_free, last_a - len(LATE) + 1)
                chain(mxa[:, :, :], 0)

                def body(i, s, ip, last):
                    for e in range(NSTEP):
                        if e == 3:
                            pool.wait_ge(mxb_done, i + 1)
                            pool.wait_ge(s_full[0], USES * i + 1)
                            chain(mxb[:, 0, :, :], 2 * i + 1)
                            job(3 * ip + s + (s == 1))
                        if e == DA_AT - 1 and not last:
                            pool.wait_ge(m_free, PREP + NPC * i + last_a + 1)
                            pool.wait_ge(s_full[0], full(i, DB_USE, 0))
                            chain(mxa[:, :, :], 2 * i + 2)
                        if e == DA_AT and s == 0:
                            job(3 * ip + 1)
                groups(pool, body)

            @block.scalar
            def _(act):
                def copy_d(b, count):
                    act.wait_ge(s_full[0], count)
                    act.activation(dt_sb[b][:, :], pair[0][0:48, 0, 0:P // 2].bitcast(BF16), ACT.Copy).then_inc(d_copied, 1)

                def exps(i, e, p, last):
                    w = 512 - STEPS[e][2]
                    act.wait_ge(s_full[p], full(i, use(e, p, last), p))
                    act.wait_ge(pv_done, NSTEP * i + e + 1)
                    act.activation(pr[e % 3][:, 2 * p:2 * p + 2, 0:w], pair[p][:, :, 0:w], ACT.Exp, scale=SCALE)\
                       .then_inc(exp_done, 1)

                def copy_o(i, qb):
                    act.wait_ge(pv_done, PV0 + NSTEP * i + (4, NSTEP)[qb])
                    act.activation(ot[:, :], b_o[:, :], ACT.Copy).then_inc(ot_done, 1)

                def convert(jj):
                    w = w_f[:, bass.ds(jj * HALF, HALF)]
                    act.wait_ge(z_in, 32 * jj + 32)
                    act.activation(w, w.bitcast(I32), ACT.Copy)
                    act.activation(zst[:, :], zst[:, :].bitcast(I32), ACT.Copy).then_inc(z_conv, 1)

                act.wait_ge(w_in, 16 * JOBS)
                copy_d(0, 1)

                def body(i, s, ip, last):
                    for e in range(NSTEP):
                        if e == 4:
                            copy_d(1, full(i, DB_USE, 0))
                            copy_o(i, 0)
                            convert(3 * ip + s + (s == 1))
                        if e == DA_AT + 1:
                            if not last:
                                copy_d(0, full(i, DA_USE, 0))
                            if s == 0:
                                convert(3 * ip + 1)
                        exps(i, e, 0, last)
                        exps(i, e, 1, last)
                    copy_o(i, 1)
                groups(act, body)

            @block.vector
            def _(dve):
                def take(pc, n):
                    qt, j, k0, w = pc
                    src = b_m[n_slot(pc)][:, 0:w]
                    dst = mxa[:, j, qt:qt + 1] if qt < 4 else mxb[:, k0 // 512, j, qt - 4:qt - 3]
                    dve.wait_ge(m_full, n + 1)
                    if k0 + w == (qt + 1) * P:
                        apart(dve, "dve")
                        dve.tensor_tensor_reduce(out=src, in0=src, in1=tri[:, 512 - w:512], scale=1.0,
                                                 scalar=-3.0e38, op0=ALU.add, op1=ALU.max, accum_out=dst).then_inc(m_free, 1)
                    else:
                        dve.tensor_reduce(dst, src, AX.X, ALU.max).then_inc(m_free, 1)

                def normalise(i, qb):
                    n = (O0_USE, O1_USE)[qb]
                    dve.wait_ge(s_full[1], full(i, n, 1))
                    src = pair[1][:, 0, :].rearrange("p (t j w) -> p t j w", t=4, j=GH)
                    dve.reciprocal(rec[:, :, :], src[:, :, :, HD]).then_inc(rec_done, 1)
                    dve.wait_ge(rec_done, 2 * i + qb + 1)
                    dst = o_sb[:, bass.ds(i, 1), 4 * qb:4 * qb + 4, :].rearrange("p a t (j d) -> p (a t) j d", j=GH)
                    dve.tensor_tensor(dst, src[:, :, :, 0:HD], rec[:, :, :].unsqueeze(3).to_broadcast([P, 4, GH, HD]),
                                      ALU.mult).then_inc(s_free[1], 1)

                def lot(i, pcs):
                    for pc in pcs:
                        n = PREP + NPC * i + number[pc]
                        if pc == EARLY[0]:
                            dve.wait_ge(d_chain, 10 * i + 1)
                        if pc[0] == 4 and pc == next(x for x in EARLY if x[0] == 4):
                            dve.wait_ge(d_chain, 10 * i + 6)
                        take(pc, n)

                dve.memset(b_o[:, :], 0.0).then_inc(o_clear, 1)
                dve.wait_ge(tri_done, 16)
                for pc in EARLY:
                    take(pc, number[pc] - len(LATE))

                def body(i, s, ip, last):
                    for e in range(NSTEP):
                        if e == 4:
                            dve.wait_ge(m_free, PREP + NPC * i + len(LATE))
                            dve.tensor_tensor(mxb[:, 0, :, :], mxb[:, 0, :, :], mxb[:, 1, :, :], ALU.max).then_inc(mxb_done, 1)
                            if not last:
                                lot(i, EARLY[0:GAP])
                        if not last or e < 4:
                            lot(i, plan[2 * e])
                        if e == O0_AT + 1:
                            normalise(i, 0)
                        if not last or e < 4:
                            lot(i, plan[2 * e + 1])
                    if not last:
                        lot(i, EARLY[-HELD:])
                    normalise(i, 1)
                groups(dve, body)

            @block.tensor
            def _(pe):
                def score(s, pc, n):
                    qt, j, k0, w = pc
                    if not (isinstance(n, int) and n < 3):
                        pe.wait_ge(m_free, n - 2)
                    pe.matmul(b_m[n_slot(pc)][:, 0:w], qs[s][0:ROWS_MAX, qt // 4, j, (qt % 4) * P:(qt % 4 + 1) * P],
                              ks[s][0:ROWS_MAX, k0 // 512, j, 0:w], start=True, stop=True).then_inc(m_full, 1)

                def lot(i, s, pcs):
                    for pc in pcs:
                        score(s if pc in LATE else 1 - s, pc, PREP + NPC * i + number[pc])

                def trans_d(n, free):
                    if free is not None:
                        pe.wait_ge(*free)
                    pe.wait_ge(d_chain, 5 * n + 5)
                    apart(pe, "pe")
                    pe.transpose(pair[0][0:48, 0, 0:P // 2].bitcast(BF16), d3[:, :, :].rearrange("p a b -> p (a b)"),
                                 identb[:, :]).then_inc(s_full[0], 1)

                def slot0_free(i, n, last):
                    if n == 0:
                        pe.wait_ge(exp_done, EX + 2 * NSTEP * i - 1)
                    elif n == DB_USE + 1:
                        pe.wait_ge(d_copied, 2 * i + 2)
                    elif n == DA_USE + 1 and not last:
                        pe.wait_ge(d_copied, 2 * i + 3)
                    else:
                        e = n - 1 - (n - 1 > DB_USE) - (n - 1 > DA_USE and not last)
                        pe.wait_ge(exp_done, EX + 2 * NSTEP * i + 2 * e + 1)

                def second(i, s, e, p):
                    qb, kt, c0 = STEPS[e]
                    for jj in range(2):
                        j = 2 * p + jj
                        mm = pe.matmul(pair[p][:, jj, 0:512 - c0], ks[s][0:ROWS, kt // 4, j, (kt % 4) * P:(kt % 4 + 1) * P],
                                       qs[s][0:ROWS, qb, j, c0:512], start=True, stop=not diag[e])
                    if diag[e]:
                        for jj in range(2):
                            mm = pe.matmul(pair[p][:, jj, 0:P], identb[:, :], behind[:, :], start=False, stop=True)
                    mm.then_inc(s_full[p], 1)

                def pv(i, s, e):
                    qb, kt, c0 = STEPS[e]
                    pe.wait_ge(exp_done, EX + 2 * NSTEP * i + 2 * e + 2)
                    if kt == 0:
                        pe.wait_ge(ot_done, EXTRA + 2 * i + qb)
                    for j in range(GH):
                        mm = pe.matmul(b_o[32 * j:32 * j + VW, c0:512], vs[s][:, kt, j * VW:(j + 1) * VW],
                                       pr[e % 3][:, j, 0:512 - c0], start=(kt == 0), stop=(kt == 4 * qb + 3),
                                       tile_position=(0, 32 * j))
                    mm.then_inc(pv_done, 1)

                def trans_o(i, qb):
                    pe.wait_ge(ot_done, EXTRA + 2 * i + qb + 1)
                    e = (O0_AT, NSTEP - 1)[qb]
                    pe.wait_ge(exp_done, EX + 2 * NSTEP * i + 2 * e + 2)
                    for t in range(4):
                        mm = pe.transpose(pair[1][:, 0, t * P:(t + 1) * P], ot[:, t * P:(t + 1) * P], ident[:, :])
                    mm.then_inc(s_full[1], 1)

                pe.wait_ge(stk_in[0], 144)
                for pc in EARLY:
                    score(0, pc, number[pc] - len(LATE))
                trans_d(0, None)
                pe.wait_ge(o_clear, 1)
                pe.wait_ge(mask_in, 16)

                def body(i, s, ip, last):
                    for e in range(NSTEP):
                        if e == 0:
                            pe.wait_ge(da_in, 16 * i + 16)
                        if e == 4:
                            if not last:
                                pe.wait_ge(stk_in[1 - s], 144 * (ip + 1 + s))
                                lot(i, s, EARLY[0:GAP])
                            pv(i, s, 3)
                            trans_d(2 * i + 1, (exp_done, EX + 2 * NSTEP * i + 7))
                            pe.wait_ge(db_in, 16 * i + 16)
                        slot0_free(i, use(e, 0, last), last)
                        second(i, s, e, 0)
                        if not last or e < 4:
                            lot(i, s, plan[2 * e])
                        slot1_free(i, e)
                        second(i, s, e, 1)
                        if not last or e < 4:
                            lot(i, s, plan[2 * e + 1])
                        if e not in (0, 4):
                            pv(i, s, e - 1)
                        if e == O0_AT:
                            trans_o(i, 0)
                        if e == DA_AT and not last:
                            trans_d(2 * i + 2, (exp_done, EX + 2 * NSTEP * i + 2 * e + 1))
                    pv(i, s, NSTEP - 1)
                    if not last:
                        lot(i, s, EARLY[-HELD:])
                    trans_o(i, 1)

                def slot1_free(i, e):
                    if e == 0:
                        pe.wait_ge(s_free[1], EXTRA + 2 * i)
                    elif e == O0_AT + 1:
                        pe.wait_ge(s_free[1], EXTRA + 2 * i + 1)
                    else:
                        pe.wait_ge(exp_done, EX + 2 * NSTEP * i + 2 * e)
                groups(pe, body)

        def w_cols(n, it):
            rows = w_f[:, n * KT * INNER:(n + 1) * KT * INNER].rearrange("p (k c) -> p k c", k=KT)
            return rows[:, :, it * P:(it + 1) * P]

        def w_down(it):
            return w_f[:, 2 * KT * INNER + it * D:2 * KT * INNER + (it + 1) * D]

        xc_in, xuse_d, xuse_p = [S(f"xc_in{n}") for n in range(2)], S("xuse_d"), S("xuse_p")
        o_in, o_tr, o_hi, o_lo, s_proj, s_cp = S("o_in"), S("o_tr"), S("o_hi"), S("o_lo"), S("s_proj"), S("s_cp")
        xc_tr, xc_h, xc_l = S("xc_tr"), S("xc_h"), S("xc_l")
        wg_hi, wg_lo, wd_hi, wd_lo = S("wg_hi"), S("wg_lo"), S("wd_hi"), S("wd_lo")
        gu_done, silu_done, h_mul, hh_done, hl_done, down_done = (
            S("gu_done"), S("silu_done"), S("h_mul"), S("hh_done"), S("hl_done"), S("down_done"))
        y_silu, y_mul, o_stored = S("y_silu"), S("y_mul"), [S(f"o_stored{n}") for n in range(2)]
        y = bank
        NB = TOK // 512
        C_P, C_OTR, C_OLO, C_YS, C_YM, C_XTR, C_XL, C_H, C_HL, C_ST = 4, 1, 2, 4, 4, 1, 2, 2, 2, 16

        with nc.Block() as block:
            @block.sync
            def _(sp):
                with sp.Fori(0, NB) as blk:
                    for u in range(4):
                        if u < 2:
                            sp.wait_ge(xuse_p, 4 * blk + u + 3)
                        else:
                            sp.wait_ge(xuse_d, 4 * blk + u - 1)
                        sp.dma_start(xin_c[:, u % 2, :], x_t[4 * blk + u]).then_inc(xc_in[u % 2], 16)
                    for u in range(4):
                        if u < 2:
                            sp.wait_ge(xuse_d, 4 * blk + u + 3)
                        else:
                            sp.wait_ge(xuse_p, C_P + 4 * blk + u - 1)
                            sp.dma_start(out_t[4 * blk + u - 2], ost[:, u % 2, :]).then_inc(o_stored[u % 2], 16)
                        sp.dma_start(xin_c[:, u % 2, :], x_t[4 * blk + u]).then_inc(xc_in[u % 2], 16)
                    for u in range(2, 4):
                        sp.wait_ge(xuse_p, C_P + 4 * blk + u + 1)
                        sp.dma_start(out_t[4 * blk + u], ost[:, u % 2, :]).then_inc(o_stored[u % 2], 16)
                for n in range(2):
                    sp.wait_ge(o_stored[n], C_ST + 8 * TILES)

            @block.gpsimd
            def _(pool):
                for s_, n in ((xuse_p, C_P), (o_tr, C_OTR), (o_lo, C_OLO), (y_silu, C_YS), (y_mul, C_YM),
                              (xc_tr, C_XTR), (xc_l, C_XL), (h_mul, C_H), (hl_done, C_HL), (o_stored[0], C_ST), (o_stored[1], C_ST)):
                    pool.sem_inc(s_, n)

                def low(dst, src, hi):
                    return pool.tensor_tensor(dst, src, hi.bitcast(F32), ALU.subtract)

                def w_gu(blk, it):
                    s = it % 2
                    pool.wait_ge(wg_hi, IT * blk + it + 1)
                    for n in range(2):
                        mm = low(ws_lo[s][:, n, :].rearrange("p (k c) -> p k c", k=KT), w_cols(n, it),
                                 ws_hi[s][:, n, :].rearrange("p (k c) -> p k c", k=KT))
                    mm.then_inc(wg_lo, 1)

                def w_d(blk, it):
                    s = it % 2
                    pool.wait_ge(wd_hi, IT * blk + it + 1)
                    low(ws_lo[s][:, 2, :], w_down(it), ws_hi[s][:, 2, :]).then_inc(wd_lo, 1)

                with pool.Fori(0, NB) as blk:
                    w_gu(blk, 0)
                    w_gu(blk, 1)
                    w_d(blk, 0)
                    for it in range(IT):
                        if it + 2 < IT:
                            w_gu(blk, it + 2)
                        if it + 1 < IT:
                            w_d(blk, it + 1)
                    for u in range(4):
                        pool.wait_ge(y_mul, C_YM + 4 * blk + u + 1)
                        pool.wait_ge(xc_in[u % 2], 64 * blk + 16 * (u // 2 + 3))
                        pool.tensor_tensor(ost[:, u % 2, :], ost[:, u % 2, :], xin_c[:, u % 2, :], ALU.add).then_inc(xuse_p, 1)

            @block.scalar
            def _(act):
                def copy(dst, src):
                    return act.activation(dst, src, ACT.Copy)

                def load_o(blk, u):
                    act.wait_ge(o_tr, 4 * blk + u + 1)
                    t = 4 * blk + u
                    src = o_sb[:, bass.ds((t // QT) * GROUPS, GROUPS), bass.ds(t % QT, 1), :]
                    copy(oin[:, :].rearrange("p (g a w) -> p g a w", g=GROUPS, a=1), src).then_inc(o_in, 1)

                def hi_o(blk, u):
                    act.wait_ge(o_tr, C_OTR + 4 * blk + u + 1)
                    copy(h_hi[u % 2][:, :], pair[0][:, u % 2, :]).then_inc(o_hi, 1)

                def hi_x(blk, u):
                    act.wait_ge(xc_tr, C_XTR + 4 * blk + u + 1)
                    copy(xc_hi[:, :, u * P:(u + 1) * P], pair[1][:, u % 2, :].rearrange("p (k c) -> p k c", k=KT)).then_inc(xc_h, 1)

                def copy_s(blk, u):
                    act.wait_ge(s_proj, 4 * blk + u + 1)
                    act.wait_ge(y_mul, 4 * blk + u + 1)
                    copy(s_sb[:, u, :], y[u][:, :]).then_inc(s_cp, 1)

                def w_gu(blk, it):
                    for n in range(2):
                        mm = copy(ws_hi[it % 2][:, n, :].rearrange("p (k c) -> p k c", k=KT), w_cols(n, it))
                    mm.then_inc(wg_hi, 1)

                def w_d(blk, it):
                    if it > 1:
                        act.wait_ge(down_done, IT * blk + it - 1)
                    copy(ws_hi[it % 2][:, 2, :], w_down(it)).then_inc(wd_hi, 1)

                with act.Fori(0, NB) as blk:
                    load_o(blk, 0)
                    w_gu(blk, 0)
                    load_o(blk, 1)
                    hi_o(blk, 0)
                    hi_o(blk, 1)
                    hi_x(blk, 0)
                    load_o(blk, 2)
                    copy_s(blk, 0)
                    hi_o(blk, 2)
                    hi_x(blk, 1)
                    load_o(blk, 3)
                    copy_s(blk, 1)
                    hi_o(blk, 3)
                    hi_x(blk, 2)
                    copy_s(blk, 2)
                    hi_x(blk, 3)
                    w_gu(blk, 1)
                    w_d(blk, 0)
                    copy_s(blk, 3)
                    for it in range(IT):
                        act.wait_ge(gu_done, IT * blk + it + 1)
                        act.wait_ge(hl_done, IT * blk + it + 1)
                        act.activation(sg[it % 2][:, :], pair[it % 2][:, 0, :], ACT.Silu).then_inc(silu_done, 1)
                        if it + 2 < IT:
                            w_gu(blk, it + 2)
                        act.wait_ge(h_mul, C_H + IT * blk + it + 1)
                        if it > 1:
                            act.wait_ge(down_done, IT * blk + it - 1)
                        copy(h_hi[it % 2][:, :], sg[it % 2][:, :]).then_inc(hh_done, 1)
                        if it + 1 < IT:
                            w_d(blk, it + 1)
                    act.wait_ge(down_done, IT * blk + IT)
                    for u in range(4):
                        if u > 1:
                            act.wait_ge(y_mul, C_YM + 4 * blk + u - 1)
                        act.activation(sg[u % 2][:, :], y[u][:, :], ACT.Silu).then_inc(y_silu, 1)

            @block.vector
            def _(dve):
                def norm(blk, u):
                    t = 4 * blk + u
                    dve.wait_ge(xc_in[u % 2], 64 * blk + 16 * (u // 2 + 1))
                    dve.wait_ge(xc_tr, 4 * blk + u + 1)
                    dve.tensor_scalar(xnc[:, :], xin_c[:, u % 2, :], xmean[:, bass.ds(t, 1)], xrstd[:, bass.ds(t, 1)],
                                      ALU.subtract, ALU.mult).then_inc(xuse_d, 1)

                def lo_o(blk, u):
                    dve.wait_ge(o_hi, 4 * blk + u + 1)
                    dve.tensor_tensor(h_lo[u % 2][:, :], pair[0][:, u % 2, :], h_hi[u % 2][:, :].bitcast(F32), ALU.subtract)\
                       .then_inc(o_lo, 1)

                def lo_x(blk, u):
                    dve.wait_ge(xc_h, 4 * blk + u + 1)
                    cols = slice(u * P, (u + 1) * P)
                    dve.tensor_tensor(xc_lo[:, :, cols], pair[1][:, u % 2, :].rearrange("p (k c) -> p k c", k=KT),
                                      xc_hi[:, :, cols].bitcast(F32), ALU.subtract).then_inc(xc_l, 1)

                with dve.Fori(0, NB) as blk:
                    norm(blk, 0)
                    lo_o(blk, 0)
                    lo_o(blk, 1)
                    lo_x(blk, 0)
                    norm(blk, 1)
                    lo_o(blk, 2)
                    lo_x(blk, 1)
                    norm(blk, 2)
                    lo_o(blk, 3)
                    lo_x(blk, 2)
                    norm(blk, 3)
                    lo_x(blk, 3)
                    for it in range(IT):
                        s = it % 2
                        dve.wait_ge(silu_done, IT * blk + it + 1)
                        dve.tensor_tensor(sg[s][:, :], pair[s][:, 1, :], sg[s][:, :], ALU.mult).then_inc(h_mul, 1)
                        dve.wait_ge(hh_done, IT * blk + it + 1)
                        dve.tensor_tensor(h_lo[s][:, :], sg[s][:, :], h_hi[s][:, :].bitcast(F32), ALU.subtract).then_inc(hl_done, 1)
                    for u in range(4):
                        dve.wait_ge(y_silu, C_YS + 4 * blk + u + 1)
                        dve.wait_ge(o_stored[u % 2], 32 * blk + 16 * (u // 2) + 16)
                        dve.tensor_tensor(ost[:, u % 2, :], sg[u % 2][:, :], s_sb[:, u, :], ALU.mult).then_inc(y_mul, 1)

            @block.tensor
            def _(pe):
                def trans_o(blk, u):
                    pe.wait_ge(o_in, 4 * blk + u + 1)
                    pe.wait_ge(o_lo, 4 * blk + u + 1)
                    for k in range(KT):
                        mm = pe.transpose(pair[0][:, u % 2, k * P:(k + 1) * P], oin[:, k * P:(k + 1) * P], ident[:, :])
                    mm.then_inc(o_tr, 1)

                def trans_x(blk, u):
                    pe.wait_ge(xuse_d, 4 * blk + u + 1)
                    pe.wait_ge(xc_l, 4 * blk + u + 1)
                    for k in range(KT):
                        mm = pe.transpose(pair[1][:, u % 2, k * P:(k + 1) * P], xnc[:, k * P:(k + 1) * P], ident[:, :])
                    mm.then_inc(xc_tr, 1)

                def terms(l_hi, l_lo, r_hi, r_lo):
                    return (l_lo, r_hi), (l_hi, r_lo), (l_hi, r_hi)

                def s_project(blk, u):
                    pe.wait_ge(o_lo, C_OLO + 4 * blk + u + 1)
                    pe.wait_ge(y_silu, 4 * blk + u + 1)
                    for k in range(KT):
                        cols = slice(k * P, (k + 1) * P)
                        for n, (l, r) in enumerate(terms(h_hi[u % 2][:, cols], h_lo[u % 2][:, cols], wo_hi[:, k, :], wo_lo[:, k, :])):
                            mm = pe.matmul(y[u][:, :], l, r, start=(k == 0 and n == 0), stop=(k == KT - 1 and n == 2))
                    mm.then_inc(s_proj, 1)

                def gate_up(blk, it):
                    s = it % 2
                    if it == 0:
                        pe.wait_ge(xc_l, C_XL + 4 * blk + 4)
                    pe.wait_ge(wg_lo, IT * blk + it + 1)
                    pe.wait_ge(h_mul, IT * blk + it + 1)
                    for g in range(2):
                        for k in range(KT):
                            cols = slice(k * P, (k + 1) * P)
                            for n, (l, r) in enumerate(terms(ws_hi[s][:, g, cols], ws_lo[s][:, g, cols], xc_hi[:, k, :], xc_lo[:, k, :])):
                                mm = pe.matmul(pair[s][:, g, :], l, r, start=(k == 0 and n == 0), stop=(k == KT - 1 and n == 2))
                    mm.then_inc(gu_done, 1)

                def down(blk, it):
                    s = it % 2
                    if it == 0:
                        pe.wait_ge(s_cp, 4 * blk + 4)
                    pe.wait_ge(wd_lo, IT * blk + it + 1)
                    pe.wait_ge(hl_done, C_HL + IT * blk + it + 1)
                    for t in range(4):
                        cols = slice(t * P, (t + 1) * P)
                        for n, (l, r) in enumerate(terms(h_hi[s][:, cols], h_lo[s][:, cols], ws_hi[s][:, 2, :], ws_lo[s][:, 2, :])):
                            mm = pe.matmul(y[t][:, :], l, r, start=(it == 0 and n == 0), stop=(it == IT - 1 and n == 2))
                    mm.then_inc(down_done, 1)

                with pe.Fori(0, NB) as blk:
                    trans_o(blk, 0)
                    trans_o(blk, 1)
                    trans_x(blk, 0)
                    s_project(blk, 0)
                    trans_o(blk, 2)
                    trans_x(blk, 1)
                    s_project(blk, 1)
                    trans_o(blk, 3)
                    trans_x(blk, 2)
                    s_project(blk, 2)
                    trans_x(blk, 3)
                    s_project(blk, 3)
                    gate_up(blk, 0)
                    for it in range(IT):
                        if it + 1 < IT:
                            gate_up(blk, it + 1)
                        down(blk, it)


def _constants():
    import numpy as np

    def bits(a):
        return (np.ascontiguousarray(a, np.float32).view(np.uint32) >> 16).astype(np.uint16)

    def bf(a):
        u = np.ascontiguousarray(a, np.float32).view(np.uint32).astype(np.uint64)
        return ((u + 0x7FFF + ((u >> 16) & 1)) & 0xFFFF0000).astype(np.uint32).view(np.float32)
    eye = np.eye(P, dtype=np.float32)
    tri = np.zeros((P, 512), np.float32)
    tri[:, 512 - P:] = np.where(np.arange(P)[None, :] <= np.arange(P)[:, None], 0.0, -1e30)
    behind = np.where(np.arange(P)[:, None] > np.arange(P)[None, :], -1e30, 0.0).astype(np.float32)
    m = np.arange(1, HEADS + 1, dtype=np.float32) * (8.0 / HEADS)
    slope = ((1.0 / np.power(2.0, m)) / SCALE).astype(np.float32)
    h = bf(slope)
    mid = bf(slope - h)
    low = bf(slope - h - mid)
    pos = np.arange(SEQ)
    far, near, one = (pos // P * P).astype(np.float32), (pos % P).astype(np.float32), np.ones(SEQ, np.float32)
    q = np.zeros((HEADS, 12, SEQ), np.float32)
    k = np.zeros((HEADS, 15, SEQ), np.float32)
    for n in range(HEADS):
        for i, part in enumerate((h[n], mid[n], low[n])):
            q[n, 4 * i:4 * i + 4] = part * one, -far, part * one, -near
            k[n, 4 * i:4 * i + 4] = far, part * one, near, part * one
        k[n, 12:] = 1.0

    def rows(a):
        return bits(a.reshape(GROUPS, GH, -1, 2, 512).transpose(0, 2, 3, 1, 4).reshape(GROUPS, -1, GH * SEQ))
    return {"ident": eye, "identb": bits(eye), "tri": tri, "behind": bits(behind), "qrows": rows(q), "krows": rows(k)}


def kernel(L0_attn_hidden_states, L0_attn_Wqkv, L0_attn_q_ln_w, L0_attn_q_ln_b, L0_attn_k_ln_w, L0_attn_k_ln_b,
           L0_attn_Wout, L0_ffn_gate_w, L0_ffn_gate_z, L0_ffn_gate_s, L0_ffn_up_w, L0_ffn_up_z, L0_ffn_up_s,
           L0_ffn_down_w, L0_ffn_down_z, L0_ffn_down_s):
    import numpy as np
    import concourse.bacc as bacc
    from concourse.bass_utils import run_bass_kernel_spmd as run

    A = np.asarray

    def packed(gate, up, down, rows):
        d = A(down).reshape(IT, rows, D).transpose(1, 0, 2).reshape(rows, KT, INNER).transpose(1, 0, 2)
        return np.ascontiguousarray(np.concatenate([A(gate).reshape(KT, rows, INNER), A(up).reshape(KT, rows, INNER), d]))
    wproj = np.concatenate([A(L0_attn_Wqkv).T, A(L0_attn_Wout).T], axis=1).reshape(KT, P, 4 * D)
    arrays = {
        "x": A(L0_attn_hidden_states),
        "wproj": np.ascontiguousarray(wproj),
        "lnw": np.stack([A(L0_attn_q_ln_w), A(L0_attn_q_ln_b), A(L0_attn_k_ln_w), A(L0_attn_k_ln_b)]),
        "w_all": packed(L0_ffn_gate_w, L0_ffn_up_w, L0_ffn_down_w, P),
        "z_all": packed(L0_ffn_gate_z, L0_ffn_up_z, L0_ffn_down_z, 1).reshape(NHALF, HALF),
        "s_all": packed(L0_ffn_gate_s, L0_ffn_up_s, L0_ffn_down_s, 1).reshape(NHALF, HALF),
        **_constants(),
    }
    nc = bacc.Bacc("TRN2", target_bir_lowering=False, num_devices=1)
    aps = {}
    for name, a in arrays.items():
        dt = BF16 if a.dtype == np.uint16 else mybir.dt.from_np(a.dtype)
        if a.dtype == np.uint16:
            aps[name] = nc.dram_tensor(f"in_{name}", a.shape, mybir.dt.from_np(a.dtype), kind="ExternalInput").ap().bitcast(BF16)
        else:
            aps[name] = nc.dram_tensor(f"in_{name}", a.shape, dt, kind="ExternalInput").ap()
    out = nc.dram_tensor("out", (BATCH, SEQ, D), F32, kind="ExternalOutput").ap()
    build(nc, aps["x"], aps["wproj"], aps["lnw"], aps["w_all"], aps["z_all"], aps["s_all"], aps["ident"],
          aps["identb"], aps["tri"], aps["behind"], aps["qrows"], aps["krows"], out)
    r = run(nc, [{f"in_{n}": a for n, a in arrays.items()}], core_ids=[0])
    return r.results[0]["out"]
```

```python
from contextlib import ExitStack

import concourse.bass as bass
from concourse import mybir

F32 = mybir.dt.float32
F32R = mybir.dt.float32r
BF16 = mybir.dt.bfloat16
I32 = mybir.dt.int32
ALU = mybir.AluOpType
ACT = mybir.ActivationFunctionType
AX = mybir.AxisListType

P = 128
BATCH, SEQ, D = 2, 1024, 512
HEADS, HD = 32, 16
INNER = 1792
TOK = BATCH * SEQ
TILES = TOK // P
KT = D // P
IT = INNER // P
GH = 4
GROUPS = HEADS // GH
NG = BATCH * GROUPS
QT = SEQ // P
VW = HD + 1
JOBS = 12
HALF = INNER // 2
NHALF = 2 * JOBS
CLIP = 8.0
EPS = 1e-5
SCALE = HD ** -0.5
ROWS_MAX = 108
ROWS = 111


def build(nc, x, wproj, lnw, w_all, z_all, s_all, ident_in, identb_in, tri_in, behind_in, qrows, krows, out):
    stk = nc.dram_tensor("stk", [2, BATCH, P, KT, 3, SEQ], BF16).ap()
    vscr = nc.dram_tensor("vscr", [BATCH, QT, P, GROUPS, GH * VW], F32).ap()

    x_t = x.rearrange("b (t p) d -> (b t) p d", p=P)
    out_t = out.rearrange("b (t p) d -> (b t) p d", p=P)

    with ExitStack() as ctx:
        def sem(name):
            return ctx.enter_context(nc.semaphore(name))

        def sb_in(c):
            return lambda name, shape, dt: c.enter_context(nc.sbuf_tensor(name, shape, dt))

        sb = sb_in(ctx)
        bank = [ctx.enter_context(nc.psum_tensor(f"bank{n}", [P, 512], F32)) for n in range(4)]
        pair = [ctx.enter_context(nc.psum_tensor(f"pair{n}", [P, 2, 512], F32)) for n in range(2)]

        w_f = sb("w_f", [P, JOBS * INNER], F32)
        wo_hi = sb("wo_hi", [P, KT, D], F32R)
        wo_lo = sb("wo_lo", [P, KT, D], F32R)
        ident = sb("ident", [P, P], F32)
        identb = sb("identb", [P, P], BF16)
        xmean = sb("xmean", [P, TILES], F32)
        xrstd = sb("xrstd", [P, TILES], F32)

        with ExitStack() as ca:
            sa = sb_in(ca)
            wq_hi = sa("wq_hi", [P, KT, 3 * D], F32R)
            wq_lo = sa("wq_lo", [P, KT, 3 * D], F32R)
            lnb = sa("lnb", [P, 4, D], F32)
            xin = sa("xin", [P, 2, D], F32)
            xn = sa("xn", [P, D], F32)
            xt_hi = sa("xt_hi", [P, 2, KT, P], F32R)
            xt_lo = sa("xt_lo", [P, 2, KT, P], F32R)
            qk = sa("qk", [P, 2, D], F32)
            res = sa("res", [P, 2, D], F32)
            parts = [sa(f"parts{n}", [P, 2, KT, 3, 2 * P], BF16) for n in range(2)]
            vst = sa("vst", [P, 2, HEADS, VW], F32)
            st6x = sa("st6x", [P, 6], F32)
            mvx = sa("mvx", [P, 2, 2], F32)
            st6q = sa("st6q", [P, 2, 6], F32)
            mvq = sa("mvq", [P, 2, 2], F32)
            vex = sa("vex", [P, 4], F32)
            rsq = sa("rsq", [P, 2], F32)
            mhalf = sa("mhalf", [P, 2], F32)

        o_sb = sb("o_sb", [P, NG, QT, GH * HD], F32)
        with ExitStack() as cb:
            sbb = sb_in(cb)
            qs = [sbb(f"qs{n}", [P, 2, GH, 512], BF16) for n in range(2)]
            ks = [sbb(f"ks{n}", [P, GH, SEQ], BF16) for n in range(2)]
            vs = [sbb(f"vs{n}", [P, QT, GH * VW], F32) for n in range(2)]
            pr = [sbb(f"pr{n}", [P, GH, 512], F32) for n in range(3)]
            ot = sbb("ot", [P, 512], F32)
            tri = sbb("tri", [P, 512], F32)
            behind = sbb("behind", [P, P], BF16)
            zst = sbb("zst", [P, HALF], F32)
            sst = sbb("sst", [P, HALF], F32)
            mx0 = sbb("mx0", [P, GH, 4], F32)
            mx1 = sbb("mx1", [P, 2, GH, 4], F32)
            dneg = sbb("dneg", [P, 16], F32)
            dres = sbb("dres", [P, 16], F32)
            d3 = sbb("d3", [P, 3, 16], BF16)
            dt_sb = [sbb(f"dt{n}", [48, P], BF16) for n in range(2)]
            rec = sbb("rec", [P, 4, GH], F32)
        with ExitStack() as cc:
            sc = sb_in(cc)
            xc_hi = sc("xc_hi", [P, KT, 512], F32R)
            xc_lo = sc("xc_lo", [P, KT, 512], F32R)
            ws_hi = [sc(f"ws_hi{n}", [P, 3, 512], F32R) for n in range(2)]
            ws_lo = [sc(f"ws_lo{n}", [P, 3, 512], F32R) for n in range(2)]
            h_hi = [sc(f"h_hi{n}", [P, 512], F32R) for n in range(2)]
            h_lo = [sc(f"h_lo{n}", [P, 512], F32R) for n in range(2)]
            sg = [sc(f"sg{n}", [P, 512], F32) for n in range(2)]
            s_sb = sc("s_sb", [P, 4, 512], F32)
            xin_c = sc("xin_c", [P, 2, D], F32)
            ost = sc("ost", [P, 2, D], F32)
            oin = sc("oin", [P, D], F32)
            xnc = sc("xnc", [P, D], F32)

        def S(name):
            return sem(name)

        passed = {kind: S(f"passed_{kind}") for kind in ("pool", "dve", "pe", "sp")}

        def apart(eng, kind):
            eng.sem_inc(passed[kind], 1)

        raw_in, x_in = [S(f"raw_in{kt}") for kt in range(KT)], [S(f"x_in{u}") for u in range(2)]
        cst_in, w_in = S("cst_in"), S("w_in")
        setup_done = S("setup_done")
        whi_done, wlo_done = S("whi_done"), S("wlo_done")
        x_stat, x_mv, x_var, x_rstd, xn_done = S("x_stat"), S("x_mv"), S("x_var"), S("x_rstd"), S("xn_done")
        xt_ps, xhi_done, xlo_done = S("xt_ps"), S("xhi_done"), S("xlo_done")
        proj_v, proj_q, proj_k = S("proj_v"), S("proj_q"), S("proj_k")
        v_clip, v_out = S("v_clip"), [S(f"v_out{u}") for u in range(2)]
        qk_clip, qk_stat, qk_mv, qk_mid = S("qk_clip"), S("qk_stat"), S("qk_mv"), S("qk_mid")
        qk_var, qk_rstd, qk_ln = S("qk_var"), S("qk_rstd"), S("qk_ln")
        qk_ps, part_h, part_r, part_m, part_l, part_out = (
            S("qk_ps"), S("part_h"), S("part_r"), S("part_m"), S("part_l"), [S(f"part_out{n}") for n in range(2)])

        LAST = TILES // 2 - 1
        WPC = 2
        b_xt, b_v, b_q, b_k = (bank[n] for n in range(4))
        b_t = [pair[0][:, n, :] for n in range(2)]

        def tile_pairs(eng, body):
            for s in range(2):
                body(s, s, 0, s == 0, False)
            with eng.Fori(1, LAST // 2) as q:
                for s in range(2):
                    body(2 * q + s, s, q, False, False)
            for s in range(2):
                body(LAST - 1 + s, s, LAST // 2, False, s == 1)

        with nc.Block() as block:
            @block.sync
            def _(sp):
                sp.dma_start(xin[:, 0, :], x_t[0]).then_inc(x_in[0], 16)
                for kt in range(KT):
                    sp.dma_start(w_f[:, kt * 2048:(kt + 1) * 2048], wproj[kt]).then_inc(raw_in[kt], 16)
                    if kt == 0:
                        sp.dma_start(ident[:, :], ident_in).then_inc(cst_in, 16)
                        sp.dma_start(identb[:, :], identb_in).then_inc(cst_in, 16)
                        sp.dma_start(xin[:, 1, :], x_t[1]).then_inc(x_in[1], 16)
                sp.dma_start(lnb[:, :, :], lnw.rearrange("(a n) d -> a n d", a=1).to_broadcast([P, 4, D]))\
                  .then_inc(cst_in, 16)

                def store_parts(c, s, need):
                    sp.wait_ge(part_l, need)
                    for a in range(2):
                        dst = stk[a, bass.ds(c // 4, 1), :, :, :, bass.ds((c % 4) * 2 * P, 2 * P)]
                        sp.dma_start(dst.rearrange("a p k w s -> (a p) (k w) s"),
                                     parts[s][:, a, :, :, :].rearrange("p k w s -> p (k w) s")).then_inc(part_out[s], 16)

                def body(c, s, q, first, last):
                    for u in range(2):
                        t = 2 * c + u
                        if not last:
                            sp.wait_ge(xn_done, t + 1)
                            sp.dma_start(xin[:, u, :], x_t[t + 2]).then_inc(x_in[u], 16)
                        sp.wait_ge(v_clip, t + 1)
                        sp.dma_start(vscr[t // QT, t % QT], vst[:, u, :, :].rearrange("p (g h) w -> p g (h w)", g=GROUPS))\
                          .then_inc(v_out[u], 16)
                        if u == 0 and not first:
                            store_parts(c - 1, 1 - s, 4 * c)
                    if first:
                        sp.wait_ge(wlo_done, KT)
                    if not isinstance(c, int) or WPC * c < JOBS:
                        for n in range(WPC):
                            sp.dma_start(w_f[:, bass.ds((WPC * c + n) * INNER, INNER)].bitcast(I32),
                                         w_all[bass.ds(WPC * c + n, 1)].rearrange("a p c -> (a p) c")).then_inc(w_in, 16)
                tile_pairs(sp, body)
                store_parts(LAST, 1, 2 * TILES)
                sp.wait_ge(v_out[0], 8 * TILES)
                sp.wait_ge(v_out[1], 8 * TILES)
                for n in range(2):
                    sp.wait_ge(part_out[n], 16 * (LAST + 1))

            @block.gpsimd
            def _(pool):
                pool.memset(mhalf[:, :], -0.5).then_inc(setup_done, 1)
                pool.memset(vst[:, :, :, :], 1.0).then_inc(setup_done, 1)
                pool.wait_ge(setup_done, 2)

                def x_rs(t, u):
                    pool.wait_ge(x_mv, t + 1)
                    apart(pool, "pool")
                    pool.tensor_scalar(vex[:, 0:1], mvx[:, u, 1:2], EPS, None, ALU.add).then_inc(x_var, 1)
                    pool.wait_ge(x_var, t + 1)
                    apart(pool, "pool")
                    pool.tensor_tensor(xrstd[:, bass.ds(t, 1)], vex[:, 0:1], mhalf[:, 0:1], ALU.pow).then_inc(x_rstd, 1)

                def qk_rs(t):
                    pool.wait_ge(qk_mv, 2 * t + 2)
                    apart(pool, "pool")
                    pool.tensor_scalar(vex[:, 2:4], mvq[:, :, 1], EPS, None, ALU.add).then_inc(qk_var, 1)
                    pool.wait_ge(qk_var, t + 1)
                    pool.tensor_tensor(rsq[:, :], vex[:, 2:4], mhalf[:, :], ALU.pow).then_inc(qk_rstd, 1)

                def low(t, u, s):
                    for a in range(2):
                        pool.wait_ge(part_m, 2 * t + a + 1)
                        pool.tensor_tensor(parts[s][:, a, :, 2, u * P:(u + 1) * P],
                                           res[:, a, :].rearrange("p (k s) -> p k s", k=KT),
                                           parts[s][:, a, :, 1, u * P:(u + 1) * P], ALU.subtract).then_inc(part_l, 1)
                x_rs(0, 0)
                x_rs(1, 1)

                def body(c, s, q, first, last):
                    for u in range(2):
                        t = 2 * c + u
                        if not (first and u == 0):
                            qk_rs(t - 1)
                        if not last:
                            x_rs(t + 2, u)
                        if not (first and u == 0):
                            low(t - 1, 1 - u, s if u == 1 else 1 - s)
                tile_pairs(pool, body)
                qk_rs(TILES - 1)
                low(TILES - 1, 1, 1)

            @block.scalar
            def _(act):
                for kt in range(KT):
                    act.wait_ge(raw_in[kt], 16)
                    raw = w_f[:, kt * 2048:(kt + 1) * 2048]
                    act.activation(wq_hi[:, kt, :], raw[:, 0:3 * D], ACT.Copy)
                    act.activation(wo_hi[:, kt, :], raw[:, 3 * D:], ACT.Copy).then_inc(whi_done, 1)

                def x_hi(t, u):
                    act.wait_ge(xt_ps, t + 1)
                    if not (isinstance(t, int) and t < 2):
                        act.wait_ge(proj_k, t - 1)
                    act.activation(xt_hi[:, u, :, :].rearrange("p k s -> p (k s)"), b_xt[:, :], ACT.Copy)\
                       .then_inc(xhi_done, 1)

                def high(t, u, a, s):
                    act.wait_ge(qk_ps, 2 * t + a + 1)
                    act.activation(parts[s][:, a, :, 0, u * P:(u + 1) * P],
                                   b_t[a].rearrange("p (k s) -> p k s", k=KT), ACT.Copy).then_inc(part_h, 1)

                def mid(t, u, a, s):
                    act.wait_ge(part_r, 2 * t + a + 1)
                    act.activation(parts[s][:, a, :, 1, u * P:(u + 1) * P],
                                   res[:, a, :].rearrange("p (k s) -> p k s", k=KT), ACT.Copy).then_inc(part_m, 1)

                def split(t, u, s, stored):
                    if stored is not None:
                        act.wait_ge(part_out[s], stored)
                    high(t, u, 0, s)
                    high(t, u, 1, s)
                    mid(t, u, 0, s)
                    mid(t, u, 1, s)
                x_hi(0, 0)

                def body(c, s, q, first, last):
                    for u in range(2):
                        t = 2 * c + u
                        if not (last and u == 1):
                            x_hi(t + 1, 1 - u)
                        if not (first and u == 0):
                            split(t - 1, 1 - u, s if u == 1 else 1 - s, 16 * 2 * q if u == 1 and not (isinstance(q, int) and q == 0) else None)
                tile_pairs(act, body)
                split(TILES - 1, 1, 1, None)

            @block.vector
            def _(dve):
                def x_stats(t, u, c):
                    dve.wait_ge(x_in[u], 16 * c + 16)
                    dve.bn_stats(st6x[:, :], xin[:, u, :]).then_inc(x_stat, 1)
                    dve.wait_ge(x_stat, t + 1)
                    apart(dve, "dve")
                    dve.bn_aggr(mvx[:, u, :], st6x[:, :]).then_inc(x_mv, 1)
                    dve.wait_ge(x_mv, t + 1)
                    apart(dve, "dve")
                    dve.tensor_copy(xmean[:, bass.ds(t, 1)], mvx[:, u, 0:1])

                def x_norm(t, u):
                    dve.wait_ge(x_rstd, t + 1)
                    if not (isinstance(t, int) and t < 1):
                        dve.wait_ge(xt_ps, t)
                    dve.tensor_scalar(xn[:, :], xin[:, u, :], mvx[:, u, 0:1], xrstd[:, bass.ds(t, 1)],
                                      ALU.subtract, ALU.mult).then_inc(xn_done, 1)

                def x_lo(t, u):
                    dve.wait_ge(xhi_done, t + 1)
                    dve.tensor_tensor(xt_lo[:, u, :, :].rearrange("p k s -> p (k s)"), b_xt[:, :],
                                      xt_hi[:, u, :, :].rearrange("p k s -> p (k s)").bitcast(F32), ALU.subtract)\
                       .then_inc(xlo_done, 1)

                def clip_stats(t, a):
                    dve.wait_ge((proj_q, proj_k)[a], t + 1)
                    if not (isinstance(t, int) and t < 1):
                        dve.wait_ge(qk_ps, 2 * t - 1 + a)
                    dve.tensor_scalar(qk[:, a, :], (b_q, b_k)[a][:, :], CLIP, -CLIP, ALU.min, ALU.max).then_inc(qk_clip, 1)
                    dve.wait_ge(qk_clip, 2 * t + a + 1)
                    dve.bn_stats(st6q[:, a, :], qk[:, a, :]).then_inc(qk_stat, 1)
                    dve.wait_ge(qk_stat, 2 * t + a + 1)
                    apart(dve, "dve")
                    dve.bn_aggr(mvq[:, a, :], st6q[:, a, :]).then_inc(qk_mv, 1)

                def center(t, a):
                    dve.wait_ge(qk_mv, 2 * t + a + 1)
                    dve.scalar_tensor_tensor(out=qk[:, a, :], in0=qk[:, a, :], scalar=mvq[:, a, 0:1],
                                             in1=lnb[:, 2 * a, :], op0=ALU.subtract, op1=ALU.mult).then_inc(qk_mid, 1)

                def rescale(t, a):
                    dve.wait_ge(qk_mid, 2 * t + a + 1)
                    dve.wait_ge(qk_rstd, t + 1)
                    dve.scalar_tensor_tensor(out=qk[:, a, :], in0=qk[:, a, :], scalar=rsq[:, a:a + 1],
                                             in1=lnb[:, 2 * a + 1, :], op0=ALU.mult, op1=ALU.add).then_inc(qk_ln, 1)

                def residual(t, u, a, s):
                    dve.wait_ge(part_h, 2 * t + a + 1)
                    if not (isinstance(t, int) and t < 1):
                        dve.wait_ge(part_l, 2 * t - 1 + a)
                    dve.tensor_tensor(res[:, a, :].rearrange("p (k s) -> p k s", k=KT),
                                      b_t[a].rearrange("p (k s) -> p k s", k=KT),
                                      parts[s][:, a, :, 0, u * P:(u + 1) * P], ALU.subtract).then_inc(part_r, 1)

                x_stats(0, 0, 0)
                for kt in range(KT):
                    dve.wait_ge(whi_done, kt + 1)
                    raw = w_f[:, kt * 2048:(kt + 1) * 2048]
                    dve.tensor_tensor(wq_lo[:, kt, :], raw[:, 0:3 * D], wq_hi[:, kt, :].bitcast(F32), ALU.subtract)
                    dve.tensor_tensor(wo_lo[:, kt, :], raw[:, 3 * D:], wo_hi[:, kt, :].bitcast(F32), ALU.subtract)\
                       .then_inc(wlo_done, 1)
                    if kt == 0:
                        x_norm(0, 0)
                        x_stats(1, 1, 0)
                x_lo(0, 0)
                x_norm(1, 1)
                dve.wait_ge(setup_done, 2)
                dve.wait_ge(cst_in, 48)

                def body(c, s, q, first, last):
                    for u in range(2):
                        t = 2 * c + u
                        prev = not (first and u == 0)
                        if prev:
                            clip_stats(t - 1, 1)
                            center(t - 1, 0)
                            center(t - 1, 1)
                        if not last:
                            x_stats(t + 2, u, c + 1)
                        if prev:
                            rescale(t - 1, 0)
                            rescale(t - 1, 1)
                        dve.wait_ge(proj_v, t + 1)
                        if not first:
                            dve.wait_ge(v_out[u], 16 * c)
                        dve.tensor_scalar(vst[:, u, :, 0:HD], b_v[:, :].rearrange("p (h d) -> p h d", h=HEADS),
                                          CLIP, -CLIP, ALU.min, ALU.max).then_inc(v_clip, 1)
                        if not (last and u == 1):
                            x_lo(t + 1, 1 - u)
                        if not last:
                            x_norm(t + 2, u)
                        clip_stats(t, 0)
                        if prev:
                            residual(t - 1, 1 - u, 0, s if u == 1 else 1 - s)
                            residual(t - 1, 1 - u, 1, s if u == 1 else 1 - s)
                tile_pairs(dve, body)
                t = TILES - 1
                clip_stats(t, 1)
                for a in range(2):
                    center(t, a)
                for a in range(2):
                    rescale(t, a)
                for a in range(2):
                    residual(t, 1, a, 1)

            @block.tensor
            def _(pe):
                def x_trans(t):
                    pe.wait_ge(xn_done, t + 1)
                    if not (isinstance(t, int) and t < 1):
                        pe.wait_ge(xlo_done, t)
                    for kt in range(KT):
                        mm = pe.transpose(b_xt[:, kt * P:(kt + 1) * P], xn[:, kt * P:(kt + 1) * P], ident[:, :])
                    mm.then_inc(xt_ps, 1)

                def project(t, u, n, b, done, free):
                    pe.wait_ge(xlo_done, t + 1)
                    if not (isinstance(t, int) and t < 1):
                        pe.wait_ge(*free)
                    cols = slice(n * D, (n + 1) * D)
                    for kt in range(KT):
                        if isinstance(t, int) and t < 1 and n == 2:
                            pe.wait_ge(wlo_done, kt + 1)
                        for i, (l, r) in enumerate(((xt_lo, wq_hi), (xt_hi, wq_lo), (xt_hi, wq_hi))):
                            mm = pe.matmul(b[:, :], l[:, u, kt, :], r[:, kt, cols],
                                           start=(kt == 0 and i == 0), stop=(kt == KT - 1 and i == 2))
                    mm.then_inc(done, 1)

                def qk_trans(t):
                    for a in range(2):
                        pe.wait_ge(qk_ln, 2 * t + a + 1)
                        if not (isinstance(t, int) and t < 1):
                            pe.wait_ge(part_r, 2 * t - 1 + a)
                        for kt in range(KT):
                            mm = pe.transpose(b_t[a][:, kt * P:(kt + 1) * P], qk[:, a, kt * P:(kt + 1) * P], ident[:, :])
                        mm.then_inc(qk_ps, 1)
                pe.wait_ge(cst_in, 48)
                x_trans(0)

                def body(c, s, q, first, last):
                    for u in range(2):
                        t = 2 * c + u
                        project(t, u, 2, b_v, proj_v, (v_clip, t))
                        if not (last and u == 1):
                            x_trans(t + 1)
                        project(t, u, 0, b_q, proj_q, (qk_clip, 2 * t - 1))
                        if not (first and u == 0):
                            qk_trans(t - 1)
                        project(t, u, 1, b_k, proj_k, (qk_clip, 2 * t))
                tile_pairs(pe, body)
                qk_trans(TILES - 1)

        mask_in = S("mask_in")
        tri_done, stk_in = S("tri_done"), [S(f"stk_in{n}") for n in range(2)]
        m_full, m_free = S("m_full"), S("m_free")
        s_full, s_free = [S(f"s_full{n}") for n in range(2)], [S(f"s_free{n}") for n in range(2)]
        exp_done, pv_done = S("exp_done"), S("pv_done")
        mx1_done, d_chain, d_copied, d0_in, d1_in = S("mx1_done"), S("d_chain"), S("d_copied"), S("d0_in"), S("d1_in")
        ot_done, rec_done, o_clear = S("ot_done"), S("rec_done"), S("o_clear")
        z_in, z_conv, z_sub, z_mul = S("z_in"), S("z_conv"), S("z_sub"), S("z_mul")

        b_m, b_o = bank[0:3], bank[3]
        STEPS = [(qb, kt, max(0, (kt - 4 * qb) * P)) for qb in (1, 0) for kt in range(4 * qb + 4)]
        NSTEP = len(STEPS)
        FIRST = 8
        diag = [kt >= 4 * qb for qb, kt, _ in STEPS]

        def pieces(tiles):
            return [(qt, j, k0, min(512, (qt + 1) * P - k0))
                    for qt in tiles for j in range(GH) for k0 in range(0, (qt + 1) * P, 512)]
        EARLY, LATE = pieces(range(4, 8)), pieces(range(4))
        NPC, HEAD = len(LATE) + len(EARLY), 8
        assert NPC % 3 == 0
        number = {pc: n for n, pc in enumerate(EARLY + LATE)}

        def n_slot(pc):
            return number[pc] % 3

        def spread(lot, lo, hi):
            width = [512 - STEPS[h // 2][2] for h in range(2 * NSTEP)]
            total, work = sum(width[lo:hi]), sum(pc[3] + 60 for pc in lot)
            plan, at, passed = {h: [] for h in range(lo, hi)}, 0, 0
            for h in range(lo, hi):
                passed += width[h]
                while at < len(lot) and (h == hi - 1 or sum(pc[3] + 60 for pc in lot[:at]) < work * passed / total):
                    plan[h].append(lot[at])
                    at += 1
            return plan
        E_LO, E_HI, TAIL = 6, 20, 4
        plan = spread(LATE[HEAD:], 0, E_LO) | spread(EARLY, E_LO, E_HI) | spread(LATE[:HEAD - TAIL], E_HI, 2 * NSTEP)
        D0_AT, O1_AT = 5, 9
        USES = NSTEP + 2
        D0_USE, D1_USE, O1_USE, O0_USE = D0_AT + 1, USES - 1, O1_AT + 1, USES - 1
        EXTRA = 1
        PV0 = 3
        LOADS = 16 * 29
        def use(e, p):
            return e + (e > D0_AT) if p == 0 else e + (e > O1_AT)

        def full(i, n, p):
            return USES * i + n + (2 if p == 0 else 1)

        def groups(eng, body):
            with eng.Fori(0, NG // 2 - 1) as ip:
                for s in range(2):
                    body(2 * ip + s, s, ip, None)
            for s in range(2):
                body(NG - 2 + s, s, NG // 2 - 1, s == 1)

        with nc.Block() as block:
            @block.sync
            def _(sp):
                def load(i, s, b):
                    cols = slice(b * 512, (b + 1) * 512)
                    p0 = (i % 2) * 64
                    for r, both in enumerate(((0, 0), (1, 0), (2, 0), (0, 1), (1, 1), (0, 2))):
                        rows = slice(r * HD, (r + 1) * HD)
                        src = stk[:, bass.ds(i // GROUPS, 1), bass.ds(p0, 64), bass.ds((i % GROUPS) // 2, 1), :, :]
                        for a, dst in enumerate((qs[s][rows, b, :, :], ks[s][rows, :, cols])):
                            part = src[a].rearrange("a (j c) k w s -> w c (a j) (k s)", j=GH)[both[a]]
                            sp.dma_start(dst, part[:, :, cols]).then_inc(stk_in[s], 16)
                    g = i % GROUPS
                    sp.dma_start(qs[s][96:ROWS_MAX, b, :, :], qrows[bass.ds(g, 1), :, :, cols].rearrange("a p j s -> (a p) j s"))\
                      .then_inc(stk_in[s], 16)
                    sp.dma_start(ks[s][96:ROWS, :, cols], krows[bass.ds(g, 1), :, :, cols].rearrange("a p j s -> (a p) j s"))\
                      .then_inc(stk_in[s], 16)
                    if b == 0:
                        sp.dma_start(vs[s][:, :, :], vscr[i // GROUPS, :, :, g, :].rearrange("t p w -> p t w"))\
                          .then_inc(stk_in[s], 16)

                def half_job(jj):
                    if not (isinstance(jj, int) and jj == 0):
                        sp.wait_ge(z_mul, jj)
                    sp.dma_start(zst[:, :].bitcast(I32), z_all[bass.ds(jj, 1), :].to_broadcast([P, HALF])).then_inc(z_in, 16)
                    sp.dma_start(sst[:, :], s_all[bass.ds(jj, 1), :].to_broadcast([P, HALF])).then_inc(z_in, 16)

                for b in (1, 0):
                    load(0, 0, b)
                sp.dma_start(tri[:, :], tri_in).then_inc(tri_done, 16)
                sp.dma_start(behind[:, :], behind_in).then_inc(mask_in, 16)
                for b in (1, 0):
                    load(1, 1, b)
                half_job(0)

                def body(i, s, ip, last):
                    if s == 1:
                        half_job(3 * ip + 2)
                    if not last:
                        half_job(3 * ip + (1, 3)[s])
                    if last is None:
                        sp.wait_ge(pv_done, PV0 + NSTEP * i + FIRST)
                        apart(sp, "sp")
                        load(i + 2, s, 1)
                        sp.wait_ge(pv_done, PV0 + NSTEP * i + NSTEP)
                        apart(sp, "sp")
                        load(i + 2, s, 0)
                groups(sp, body)

            @block.gpsimd
            def _(pool):
                pool.sem_inc(s_free[1], EXTRA)
                pool.sem_inc(ot_done, EXTRA)
                pool.sem_inc(pv_done, PV0)

                def chain(mx, n):
                    apart(pool, "pool")
                    pool.tensor_scalar(dneg[:, :], mx.rearrange("p j t -> p (j t)"), -1.0, None, ALU.mult).then_inc(d_chain, 1)
                    pool.wait_ge(d_chain, 5 * n + 1)
                    apart(pool, "pool")
                    pool.tensor_copy(d3[:, 0, :], dneg[:, :]).then_inc(d_chain, 1)
                    pool.wait_ge(d_chain, 5 * n + 2)
                    pool.tensor_tensor(dres[:, :], dneg[:, :], d3[:, 0, :], ALU.subtract).then_inc(d_chain, 1)
                    pool.wait_ge(d_chain, 5 * n + 3)
                    apart(pool, "pool")
                    pool.tensor_copy(d3[:, 1, :], dres[:, :]).then_inc(d_chain, 1)
                    pool.wait_ge(d_chain, 5 * n + 4)
                    pool.tensor_tensor(d3[:, 2, :], dres[:, :], d3[:, 1, :], ALU.subtract).then_inc(d_chain, 1)

                def job(jj):
                    w = w_f[:, bass.ds(jj * HALF, HALF)]
                    pool.wait_ge(z_conv, jj + 1)
                    apart(pool, "pool")
                    pool.tensor_tensor(w, w, zst[:, :], ALU.subtract).then_inc(z_sub, 1)
                    pool.wait_ge(z_sub, jj + 1)
                    apart(pool, "pool")
                    pool.tensor_tensor(w, w, sst[:, :], ALU.mult).then_inc(z_mul, 1)

                pool.wait_ge(mx1_done, 1)
                chain(mx1[:, 0, :, :], 0)

                def body(i, s, ip, last):
                    pool.wait_ge(m_free, NPC * i + NPC)
                    pool.wait_ge(s_full[0], USES * i + 1)
                    chain(mx0[:, :, :], 2 * i + 1)
                    job(3 * ip + (0, 2)[s])
                    if not last:
                        pool.wait_ge(mx1_done, i + 2)
                        pool.wait_ge(s_full[0], full(i, D0_USE, 0))
                        chain(mx1[:, 0, :, :], 2 * i + 2)
                    if s == 0:
                        job(3 * ip + 1)
                groups(pool, body)

            @block.scalar
            def _(act):
                def send_d(s, b, n, count, done):
                    act.wait_ge(s_full[0], count)
                    act.activation(dt_sb[b][:, :], pair[0][0:48, 0, 0:P // 2].bitcast(BF16), ACT.Copy).then_inc(d_copied, 1)
                    act.wait_ge(d_copied, n)
                    act.dma_start(qs[s][ROWS_MAX:ROWS, b, :, :].rearrange("a j (t c) -> a (j t) c", c=P), dt_sb[b][:, :])\
                       .then_inc(done, 16)

                def exps(i, e, p):
                    w = 512 - STEPS[e][2]
                    act.wait_ge(s_full[p], full(i, use(e, p), p))
                    act.wait_ge(pv_done, NSTEP * i + e + 1)
                    act.activation(pr[e % 3][:, 2 * p:2 * p + 2, 0:w], pair[p][:, :, 0:w], ACT.Exp, scale=SCALE)\
                       .then_inc(exp_done, 1)

                def copy_o(i, k):
                    act.wait_ge(pv_done, PV0 + NSTEP * i + (FIRST, NSTEP)[k])
                    act.activation(ot[:, :], b_o[:, :], ACT.Copy).then_inc(ot_done, 1)

                def convert(jj):
                    w = w_f[:, bass.ds(jj * HALF, HALF)]
                    act.wait_ge(z_in, 32 * jj + 32)
                    act.activation(w, w.bitcast(I32), ACT.Copy)
                    act.activation(zst[:, :], zst[:, :].bitcast(I32), ACT.Copy).then_inc(z_conv, 1)

                act.wait_ge(w_in, 16 * JOBS)
                send_d(0, 1, 1, 1, d1_in)

                def body(i, s, ip, last):
                    for e in range(NSTEP):
                        if e == 3:
                            convert(3 * ip + (0, 2)[s])
                        if e == D0_AT + 1:
                            send_d(s, 0, 2 * i + 2, full(i, D0_USE, 0), d0_in)
                        if e == FIRST + 1:
                            copy_o(i, 0)
                        exps(i, e, 0)
                        exps(i, e, 1)
                    if not last:
                        send_d(1 - s, 1, 2 * i + 3, full(i, D1_USE, 0), d1_in)
                    copy_o(i, 1)
                    if s == 0:
                        convert(3 * ip + 1)
                groups(act, body)

            @block.vector
            def _(dve):
                def take(pc, n):
                    qt, j, k0, w = pc
                    src = b_m[n_slot(pc)][:, 0:w]
                    dst = mx0[:, j, qt:qt + 1] if qt < 4 else mx1[:, k0 // 512, j, qt - 4:qt - 3]
                    dve.wait_ge(m_full, n + 1)
                    if k0 + w == (qt + 1) * P:
                        apart(dve, "dve")
                        dve.tensor_tensor_reduce(out=src, in0=src, in1=tri[:, 512 - w:512], scale=1.0,
                                                 scalar=-3.0e38, op0=ALU.add, op1=ALU.max, accum_out=dst).then_inc(m_free, 1)
                    else:
                        dve.tensor_reduce(dst, src, AX.X, ALU.max).then_inc(m_free, 1)

                def normalise(i, k):
                    n, qb = (O1_USE, O0_USE)[k], 1 - k
                    dve.wait_ge(s_full[1], full(i, n, 1))
                    src = pair[1][:, 0, :].rearrange("p (t j w) -> p t j w", t=4, j=GH)
                    dve.reciprocal(rec[:, :, :], src[:, :, :, HD]).then_inc(rec_done, 1)
                    dve.wait_ge(rec_done, 2 * i + k + 1)
                    dst = o_sb[:, bass.ds(i, 1), 4 * qb:4 * qb + 4, :].rearrange("p a t (j d) -> p (a t) j d", j=GH)
                    dve.tensor_tensor(dst, src[:, :, :, 0:HD], rec[:, :, :].unsqueeze(3).to_broadcast([P, 4, GH, HD]),
                                      ALU.mult).then_inc(s_free[1], 1)

                def lot(g, pcs):
                    for pc in pcs:
                        if pc == EARLY[0] and not isinstance(g, int):
                            dve.wait_ge(d_chain, 10 * g - 9)
                        if pc == LATE[0] and not isinstance(g, int):
                            dve.wait_ge(d_chain, 10 * g - 4)
                        take(pc, NPC * g + number[pc])
                        if pc == EARLY[-1]:
                            dve.wait_ge(m_free, NPC * g + len(EARLY))
                            dve.tensor_tensor(mx1[:, 0, :, :], mx1[:, 0, :, :], mx1[:, 1, :, :], ALU.max).then_inc(mx1_done, 1)

                dve.memset(b_o[:, :], 0.0).then_inc(o_clear, 1)
                dve.wait_ge(tri_done, 16)
                lot(0, EARLY + LATE[:HEAD])

                def body(i, s, ip, last):
                    for e in range(NSTEP):
                        for p in range(2):
                            h = 2 * e + p
                            if p == 1 and e == O1_AT + 1:
                                normalise(i, 0)
                            if h < E_LO:
                                lot(i, plan[h])
                            elif not last:
                                lot(i + 1, plan[h])
                    if not last:
                        lot(i + 1, LATE[HEAD - TAIL:HEAD])
                    normalise(i, 1)
                groups(dve, body)

            @block.tensor
            def _(pe):
                def score(s, pc, n):
                    qt, j, k0, w = pc
                    if not (isinstance(n, int) and n < 3):
                        pe.wait_ge(m_free, n - 2)
                    pe.matmul(b_m[n_slot(pc)][:, 0:w], qs[s][0:ROWS_MAX, qt // 4, j, (qt % 4) * P:(qt % 4 + 1) * P],
                              ks[s][0:ROWS_MAX, j, k0:k0 + w], start=True, stop=True).then_inc(m_full, 1)

                def lot(g, s, pcs):
                    for pc in pcs:
                        score(s, pc, NPC * g + number[pc])

                def trans_d(n, free):
                    if free is not None:
                        pe.wait_ge(*free)
                    pe.wait_ge(d_chain, 5 * n + 5)
                    apart(pe, "pe")
                    pe.transpose(pair[0][0:48, 0, 0:P // 2].bitcast(BF16), d3[:, :, :].rearrange("p a b -> p (a b)"),
                                 identb[:, :]).then_inc(s_full[0], 1)

                def slot0_free(i, e):
                    if e == D0_AT + 1:
                        pe.wait_ge(d_copied, 2 * i + 2)
                    elif e > 0:
                        pe.wait_ge(exp_done, 2 * NSTEP * i + 2 * e - 1)

                def second(i, s, e, p):
                    qb, kt, c0 = STEPS[e]
                    for jj in range(2):
                        j = 2 * p + jj
                        mm = pe.matmul(pair[p][:, jj, 0:512 - c0], ks[s][0:ROWS, j, kt * P:(kt + 1) * P],
                                       qs[s][0:ROWS, qb, j, c0:512], start=True, stop=not diag[e])
                    if diag[e]:
                        for jj in range(2):
                            mm = pe.matmul(pair[p][:, jj, 0:P], identb[:, :], behind[:, :], start=False, stop=True)
                    mm.then_inc(s_full[p], 1)

                def pv(i, s, e):
                    qb, kt, c0 = STEPS[e]
                    pe.wait_ge(exp_done, 2 * NSTEP * i + 2 * e + 2)
                    if kt == 0:
                        pe.wait_ge(ot_done, EXTRA + 2 * i + 1 - qb)
                    for j in range(GH):
                        mm = pe.matmul(b_o[32 * j:32 * j + VW, c0:512], vs[s][:, kt, j * VW:(j + 1) * VW],
                                       pr[e % 3][:, j, 0:512 - c0], start=(kt == 0), stop=(kt == 4 * qb + 3),
                                       tile_position=(0, 32 * j))
                    mm.then_inc(pv_done, 1)

                def trans_o(i, k):
                    pe.wait_ge(ot_done, EXTRA + 2 * i + k + 1)
                    pe.wait_ge(exp_done, 2 * NSTEP * i + 2 * (O1_AT, NSTEP - 1)[k] + 2)
                    for t in range(4):
                        mm = pe.transpose(pair[1][:, 0, t * P:(t + 1) * P], ot[:, t * P:(t + 1) * P], ident[:, :])
                    mm.then_inc(s_full[1], 1)

                pe.wait_ge(stk_in[0], LOADS)
                lot(0, 0, EARLY)
                trans_d(0, None)
                lot(0, 0, LATE[:HEAD])
                pe.wait_ge(o_clear, 1)
                pe.wait_ge(mask_in, 16)

                def body(i, s, ip, last):
                    for e in range(NSTEP):
                        if e == 0:
                            pe.wait_ge(d1_in, 16 * i + 16)
                        if e == FIRST:
                            pe.wait_ge(d0_in, 16 * i + 16)
                        if 2 * e == E_LO and not last:
                            pe.wait_ge(stk_in[1 - s], LOADS * (ip + 1 + s))
                        slot0_free(i, e)
                        second(i, s, e, 0)
                        for p in range(2):
                            h = 2 * e + p
                            if p == 1:
                                slot1_free(i, e)
                                second(i, s, e, 1)
                            if h < E_LO:
                                lot(i, s, plan[h])
                            elif not last:
                                lot(i + 1, 1 - s, plan[h])
                        if e > 0:
                            pv(i, s, e - 1)
                        if e == D0_AT:
                            trans_d(2 * i + 1, (exp_done, 2 * NSTEP * i + 2 * e + 1))
                        if e == O1_AT:
                            trans_o(i, 0)
                    if not last:
                        trans_d(2 * i + 2, (exp_done, 2 * NSTEP * i + 2 * NSTEP - 1))
                    pv(i, s, NSTEP - 1)
                    if not last:
                        lot(i + 1, 1 - s, LATE[HEAD - TAIL:HEAD])
                    trans_o(i, 1)

                def slot1_free(i, e):
                    if e == 0:
                        pe.wait_ge(s_free[1], EXTRA + 2 * i)
                    elif e == O1_AT + 1:
                        pe.wait_ge(s_free[1], EXTRA + 2 * i + 1)
                    else:
                        pe.wait_ge(exp_done, 2 * NSTEP * i + 2 * e)
                groups(pe, body)

        def w_cols(n, it):
            rows = w_f[:, n * KT * INNER:(n + 1) * KT * INNER].rearrange("p (k c) -> p k c", k=KT)
            return rows[:, :, it * P:(it + 1) * P]

        def w_down(it):
            return w_f[:, 2 * KT * INNER + it * D:2 * KT * INNER + (it + 1) * D]

        xc_in, xuse_d, xuse_p = [S(f"xc_in{n}") for n in range(2)], S("xuse_d"), S("xuse_p")
        o_in, o_tr, o_hi, o_lo, s_proj, s_cp = S("o_in"), S("o_tr"), S("o_hi"), S("o_lo"), S("s_proj"), S("s_cp")
        xc_tr, xc_h, xc_l = S("xc_tr"), S("xc_h"), S("xc_l")
        wg_hi, wg_lo, wd_hi, wd_lo = S("wg_hi"), S("wg_lo"), S("wd_hi"), S("wd_lo")
        gu_done, silu_done, h_mul, hh_done, hl_done, down_done = (
            S("gu_done"), S("silu_done"), S("h_mul"), S("hh_done"), S("hl_done"), S("down_done"))
        y_silu, y_mul, o_stored = S("y_silu"), S("y_mul"), [S(f"o_stored{n}") for n in range(2)]
        y = bank
        NB = TOK // 512
        C_P, C_OTR, C_OLO, C_YS, C_YM, C_XTR, C_XL, C_H, C_HL, C_ST = 4, 1, 2, 4, 4, 1, 2, 2, 2, 16

        with nc.Block() as block:
            @block.sync
            def _(sp):
                with sp.Fori(0, NB) as blk:
                    for u in range(4):
                        if u < 2:
                            sp.wait_ge(xuse_p, 4 * blk + u + 3)
                        else:
                            sp.wait_ge(xuse_d, 4 * blk + u - 1)
                        sp.dma_start(xin_c[:, u % 2, :], x_t[4 * blk + u]).then_inc(xc_in[u % 2], 16)
                    for u in range(4):
                        if u < 2:
                            sp.wait_ge(xuse_d, 4 * blk + u + 3)
                        else:
                            sp.wait_ge(xuse_p, C_P + 4 * blk + u - 1)
                            sp.dma_start(out_t[4 * blk + u - 2], ost[:, u % 2, :]).then_inc(o_stored[u % 2], 16)
                        sp.dma_start(xin_c[:, u % 2, :], x_t[4 * blk + u]).then_inc(xc_in[u % 2], 16)
                    for u in range(2, 4):
                        sp.wait_ge(xuse_p, C_P + 4 * blk + u + 1)
                        sp.dma_start(out_t[4 * blk + u], ost[:, u % 2, :]).then_inc(o_stored[u % 2], 16)
                for n in range(2):
                    sp.wait_ge(o_stored[n], C_ST + 8 * TILES)

            @block.gpsimd
            def _(pool):
                for s_, n in ((xuse_p, C_P), (o_tr, C_OTR), (o_lo, C_OLO), (y_silu, C_YS), (y_mul, C_YM),
                              (xc_tr, C_XTR), (xc_l, C_XL), (h_mul, C_H), (hl_done, C_HL), (o_stored[0], C_ST), (o_stored[1], C_ST)):
                    pool.sem_inc(s_, n)

                def low(dst, src, hi):
                    return pool.tensor_tensor(dst, src, hi.bitcast(F32), ALU.subtract)

                def w_gu(blk, it):
                    s = it % 2
                    pool.wait_ge(wg_hi, IT * blk + it + 1)
                    for n in range(2):
                        mm = low(ws_lo[s][:, n, :].rearrange("p (k c) -> p k c", k=KT), w_cols(n, it),
                                 ws_hi[s][:, n, :].rearrange("p (k c) -> p k c", k=KT))
                    mm.then_inc(wg_lo, 1)

                def w_d(blk, it):
                    s = it % 2
                    pool.wait_ge(wd_hi, IT * blk + it + 1)
                    low(ws_lo[s][:, 2, :], w_down(it), ws_hi[s][:, 2, :]).then_inc(wd_lo, 1)

                with pool.Fori(0, NB) as blk:
                    w_gu(blk, 0)
                    w_gu(blk, 1)
                    w_d(blk, 0)
                    for it in range(IT):
                        if it + 2 < IT:
                            w_gu(blk, it + 2)
                        if it + 1 < IT:
                            w_d(blk, it + 1)
                    for u in range(4):
                        pool.wait_ge(y_mul, C_YM + 4 * blk + u + 1)
                        pool.wait_ge(xc_in[u % 2], 64 * blk + 16 * (u // 2 + 3))
                        pool.tensor_tensor(ost[:, u % 2, :], ost[:, u % 2, :], xin_c[:, u % 2, :], ALU.add).then_inc(xuse_p, 1)

            @block.scalar
            def _(act):
                def copy(dst, src):
                    return act.activation(dst, src, ACT.Copy)

                def load_o(blk, u):
                    act.wait_ge(o_tr, 4 * blk + u + 1)
                    t = 4 * blk + u
                    src = o_sb[:, bass.ds((t // QT) * GROUPS, GROUPS), bass.ds(t % QT, 1), :]
                    copy(oin[:, :].rearrange("p (g a w) -> p g a w", g=GROUPS, a=1), src).then_inc(o_in, 1)

                def hi_o(blk, u):
                    act.wait_ge(o_tr, C_OTR + 4 * blk + u + 1)
                    copy(h_hi[u % 2][:, :], pair[0][:, u % 2, :]).then_inc(o_hi, 1)

                def hi_x(blk, u):
                    act.wait_ge(xc_tr, C_XTR + 4 * blk + u + 1)
                    copy(xc_hi[:, :, u * P:(u + 1) * P], pair[1][:, u % 2, :].rearrange("p (k c) -> p k c", k=KT)).then_inc(xc_h, 1)

                def copy_s(blk, u):
                    act.wait_ge(s_proj, 4 * blk + u + 1)
                    act.wait_ge(y_mul, 4 * blk + u + 1)
                    copy(s_sb[:, u, :], y[u][:, :]).then_inc(s_cp, 1)

                def w_gu(blk, it):
                    for n in range(2):
                        mm = copy(ws_hi[it % 2][:, n, :].rearrange("p (k c) -> p k c", k=KT), w_cols(n, it))
                    mm.then_inc(wg_hi, 1)

                def w_d(blk, it):
                    if it > 1:
                        act.wait_ge(down_done, IT * blk + it - 1)
                    copy(ws_hi[it % 2][:, 2, :], w_down(it)).then_inc(wd_hi, 1)

                with act.Fori(0, NB) as blk:
                    load_o(blk, 0)
                    w_gu(blk, 0)
                    load_o(blk, 1)
                    hi_o(blk, 0)
                    hi_o(blk, 1)
                    hi_x(blk, 0)
                    load_o(blk, 2)
                    copy_s(blk, 0)
                    hi_o(blk, 2)
                    hi_x(blk, 1)
                    load_o(blk, 3)
                    copy_s(blk, 1)
                    hi_o(blk, 3)
                    hi_x(blk, 2)
                    copy_s(blk, 2)
                    hi_x(blk, 3)
                    w_gu(blk, 1)
                    w_d(blk, 0)
                    copy_s(blk, 3)
                    for it in range(IT):
                        act.wait_ge(gu_done, IT * blk + it + 1)
                        act.wait_ge(hl_done, IT * blk + it + 1)
                        act.activation(sg[it % 2][:, :], pair[it % 2][:, 0, :], ACT.Silu).then_inc(silu_done, 1)
                        if it + 2 < IT:
                            w_gu(blk, it + 2)
                        act.wait_ge(h_mul, C_H + IT * blk + it + 1)
                        if it > 1:
                            act.wait_ge(down_done, IT * blk + it - 1)
                        copy(h_hi[it % 2][:, :], sg[it % 2][:, :]).then_inc(hh_done, 1)
                        if it + 1 < IT:
                            w_d(blk, it + 1)
                    act.wait_ge(down_done, IT * blk + IT)
                    for u in range(4):
                        if u > 1:
                            act.wait_ge(y_mul, C_YM + 4 * blk + u - 1)
                        act.activation(sg[u % 2][:, :], y[u][:, :], ACT.Silu).then_inc(y_silu, 1)

            @block.vector
            def _(dve):
                def norm(blk, u):
                    t = 4 * blk + u
                    dve.wait_ge(xc_in[u % 2], 64 * blk + 16 * (u // 2 + 1))
                    dve.wait_ge(xc_tr, 4 * blk + u + 1)
                    dve.tensor_scalar(xnc[:, :], xin_c[:, u % 2, :], xmean[:, bass.ds(t, 1)], xrstd[:, bass.ds(t, 1)],
                                      ALU.subtract, ALU.mult).then_inc(xuse_d, 1)

                def lo_o(blk, u):
                    dve.wait_ge(o_hi, 4 * blk + u + 1)
                    dve.tensor_tensor(h_lo[u % 2][:, :], pair[0][:, u % 2, :], h_hi[u % 2][:, :].bitcast(F32), ALU.subtract)\
                       .then_inc(o_lo, 1)

                def lo_x(blk, u):
                    dve.wait_ge(xc_h, 4 * blk + u + 1)
                    cols = slice(u * P, (u + 1) * P)
                    dve.tensor_tensor(xc_lo[:, :, cols], pair[1][:, u % 2, :].rearrange("p (k c) -> p k c", k=KT),
                                      xc_hi[:, :, cols].bitcast(F32), ALU.subtract).then_inc(xc_l, 1)

                with dve.Fori(0, NB) as blk:
                    norm(blk, 0)
                    lo_o(blk, 0)
                    lo_o(blk, 1)
                    lo_x(blk, 0)
                    norm(blk, 1)
                    lo_o(blk, 2)
                    lo_x(blk, 1)
                    norm(blk, 2)
                    lo_o(blk, 3)
                    lo_x(blk, 2)
                    norm(blk, 3)
                    lo_x(blk, 3)
                    for it in range(IT):
                        s = it % 2
                        dve.wait_ge(silu_done, IT * blk + it + 1)
                        dve.tensor_tensor(sg[s][:, :], pair[s][:, 1, :], sg[s][:, :], ALU.mult).then_inc(h_mul, 1)
                        dve.wait_ge(hh_done, IT * blk + it + 1)
                        dve.tensor_tensor(h_lo[s][:, :], sg[s][:, :], h_hi[s][:, :].bitcast(F32), ALU.subtract).then_inc(hl_done, 1)
                    for u in range(4):
                        dve.wait_ge(y_silu, C_YS + 4 * blk + u + 1)
                        dve.wait_ge(o_stored[u % 2], 32 * blk + 16 * (u // 2) + 16)
                        dve.tensor_tensor(ost[:, u % 2, :], sg[u % 2][:, :], s_sb[:, u, :], ALU.mult).then_inc(y_mul, 1)

            @block.tensor
            def _(pe):
                def trans_o(blk, u):
                    pe.wait_ge(o_in, 4 * blk + u + 1)
                    pe.wait_ge(o_lo, 4 * blk + u + 1)
                    for k in range(KT):
                        mm = pe.transpose(pair[0][:, u % 2, k * P:(k + 1) * P], oin[:, k * P:(k + 1) * P], ident[:, :])
                    mm.then_inc(o_tr, 1)

                def trans_x(blk, u):
                    pe.wait_ge(xuse_d, 4 * blk + u + 1)
                    pe.wait_ge(xc_l, 4 * blk + u + 1)
                    for k in range(KT):
                        mm = pe.transpose(pair[1][:, u % 2, k * P:(k + 1) * P], xnc[:, k * P:(k + 1) * P], ident[:, :])
                    mm.then_inc(xc_tr, 1)

                def terms(l_hi, l_lo, r_hi, r_lo):
                    return (l_lo, r_hi), (l_hi, r_lo), (l_hi, r_hi)

                def s_project(blk, u):
                    pe.wait_ge(o_lo, C_OLO + 4 * blk + u + 1)
                    pe.wait_ge(y_silu, 4 * blk + u + 1)
                    for k in range(KT):
                        cols = slice(k * P, (k + 1) * P)
                        for n, (l, r) in enumerate(terms(h_hi[u % 2][:, cols], h_lo[u % 2][:, cols], wo_hi[:, k, :], wo_lo[:, k, :])):
                            mm = pe.matmul(y[u][:, :], l, r, start=(k == 0 and n == 0), stop=(k == KT - 1 and n == 2))
                    mm.then_inc(s_proj, 1)

                def gate_up(blk, it):
                    s = it % 2
                    if it == 0:
                        pe.wait_ge(xc_l, C_XL + 4 * blk + 4)
                    pe.wait_ge(wg_lo, IT * blk + it + 1)
                    pe.wait_ge(h_mul, IT * blk + it + 1)
                    for g in range(2):
                        for k in range(KT):
                            cols = slice(k * P, (k + 1) * P)
                            for n, (l, r) in enumerate(terms(ws_hi[s][:, g, cols], ws_lo[s][:, g, cols], xc_hi[:, k, :], xc_lo[:, k, :])):
                                mm = pe.matmul(pair[s][:, g, :], l, r, start=(k == 0 and n == 0), stop=(k == KT - 1 and n == 2))
                    mm.then_inc(gu_done, 1)

                def down(blk, it):
                    s = it % 2
                    if it == 0:
                        pe.wait_ge(s_cp, 4 * blk + 4)
                    pe.wait_ge(wd_lo, IT * blk + it + 1)
                    pe.wait_ge(hl_done, C_HL + IT * blk + it + 1)
                    for t in range(4):
                        cols = slice(t * P, (t + 1) * P)
                        for n, (l, r) in enumerate(terms(h_hi[s][:, cols], h_lo[s][:, cols], ws_hi[s][:, 2, :], ws_lo[s][:, 2, :])):
                            mm = pe.matmul(y[t][:, :], l, r, start=(it == 0 and n == 0), stop=(it == IT - 1 and n == 2))
                    mm.then_inc(down_done, 1)

                with pe.Fori(0, NB) as blk:
                    trans_o(blk, 0)
                    trans_o(blk, 1)
                    trans_x(blk, 0)
                    s_project(blk, 0)
                    trans_o(blk, 2)
                    trans_x(blk, 1)
                    s_project(blk, 1)
                    trans_o(blk, 3)
                    trans_x(blk, 2)
                    s_project(blk, 2)
                    trans_x(blk, 3)
                    s_project(blk, 3)
                    gate_up(blk, 0)
                    for it in range(IT):
                        if it + 1 < IT:
                            gate_up(blk, it + 1)
                        down(blk, it)


def _constants():
    import numpy as np

    def bits(a):
        return (np.ascontiguousarray(a, np.float32).view(np.uint32) >> 16).astype(np.uint16)

    def bf(a):
        u = np.ascontiguousarray(a, np.float32).view(np.uint32).astype(np.uint64)
        return ((u + 0x7FFF + ((u >> 16) & 1)) & 0xFFFF0000).astype(np.uint32).view(np.float32)
    eye = np.eye(P, dtype=np.float32)
    tri = np.zeros((P, 512), np.float32)
    tri[:, 512 - P:] = np.where(np.arange(P)[None, :] <= np.arange(P)[:, None], 0.0, -1e30)
    behind = np.where(np.arange(P)[:, None] > np.arange(P)[None, :], -1e30, 0.0).astype(np.float32)
    m = np.arange(1, HEADS + 1, dtype=np.float32) * (8.0 / HEADS)
    slope = ((1.0 / np.power(2.0, m)) / SCALE).astype(np.float32)
    h = bf(slope)
    mid = bf(slope - h)
    low = bf(slope - h - mid)
    pos = np.arange(SEQ)
    far, near, one = (pos // P * P).astype(np.float32), (pos % P).astype(np.float32), np.ones(SEQ, np.float32)
    q = np.zeros((HEADS, 12, SEQ), np.float32)
    k = np.zeros((HEADS, 15, SEQ), np.float32)
    for n in range(HEADS):
        for i, part in enumerate((h[n], mid[n], low[n])):
            q[n, 4 * i:4 * i + 4] = part * one, -far, part * one, -near
            k[n, 4 * i:4 * i + 4] = far, part * one, near, part * one
        k[n, 12:] = 1.0

    q = q.reshape(GROUPS, GH, 12, SEQ).transpose(0, 2, 1, 3)
    k = k.reshape(GROUPS, GH, 15, SEQ).transpose(0, 2, 1, 3)
    return {"ident": eye, "identb": bits(eye), "tri": tri, "behind": bits(behind), "qrows": bits(q), "krows": bits(k)}


def kernel(L0_attn_hidden_states, L0_attn_Wqkv, L0_attn_q_ln_w, L0_attn_q_ln_b, L0_attn_k_ln_w, L0_attn_k_ln_b,
           L0_attn_Wout, L0_ffn_gate_w, L0_ffn_gate_z, L0_ffn_gate_s, L0_ffn_up_w, L0_ffn_up_z, L0_ffn_up_s,
           L0_ffn_down_w, L0_ffn_down_z, L0_ffn_down_s):
    import numpy as np
    import concourse.bacc as bacc
    from concourse.bass_utils import run_bass_kernel_spmd as run

    A = np.asarray

    def packed(gate, up, down, rows):
        d = A(down).reshape(IT, rows, D).transpose(1, 0, 2).reshape(rows, KT, INNER).transpose(1, 0, 2)
        return np.ascontiguousarray(np.concatenate([A(gate).reshape(KT, rows, INNER), A(up).reshape(KT, rows, INNER), d]))
    wproj = np.concatenate([A(L0_attn_Wqkv).T, A(L0_attn_Wout).T], axis=1).reshape(KT, P, 4 * D)
    arrays = {
        "x": A(L0_attn_hidden_states),
        "wproj": np.ascontiguousarray(wproj),
        "lnw": np.stack([A(L0_attn_q_ln_w), A(L0_attn_q_ln_b), A(L0_attn_k_ln_w), A(L0_attn_k_ln_b)]),
        "w_all": packed(L0_ffn_gate_w, L0_ffn_up_w, L0_ffn_down_w, P),
        "z_all": packed(L0_ffn_gate_z, L0_ffn_up_z, L0_ffn_down_z, 1).reshape(NHALF, HALF),
        "s_all": packed(L0_ffn_gate_s, L0_ffn_up_s, L0_ffn_down_s, 1).reshape(NHALF, HALF),
        **_constants(),
    }
    nc = bacc.Bacc("TRN2", target_bir_lowering=False, num_devices=1)
    aps = {}
    for name, a in arrays.items():
        dt = BF16 if a.dtype == np.uint16 else mybir.dt.from_np(a.dtype)
        if a.dtype == np.uint16:
            aps[name] = nc.dram_tensor(f"in_{name}", a.shape, mybir.dt.from_np(a.dtype), kind="ExternalInput").ap().bitcast(BF16)
        else:
            aps[name] = nc.dram_tensor(f"in_{name}", a.shape, dt, kind="ExternalInput").ap()
    out = nc.dram_tensor("out", (BATCH, SEQ, D), F32, kind="ExternalOutput").ap()
    build(nc, aps["x"], aps["wproj"], aps["lnw"], aps["w_all"], aps["z_all"], aps["s_all"], aps["ident"],
          aps["identb"], aps["tri"], aps["behind"], aps["qrows"], aps["krows"], out)
    r = run(nc, [{f"in_{n}": a for n, a in arrays.items()}], core_ids=[0])
    return r.results[0]["out"]
```

```python
from contextlib import ExitStack

import concourse.bass as bass
from concourse import mybir

F32 = mybir.dt.float32
F32R = mybir.dt.float32r
BF16 = mybir.dt.bfloat16
I32 = mybir.dt.int32
ALU = mybir.AluOpType
ACT = mybir.ActivationFunctionType
AX = mybir.AxisListType

P = 128
BATCH, SEQ, D = 2, 1024, 512
HEADS, HD = 32, 16
INNER = 1792
TOK = BATCH * SEQ
TILES = TOK // P
KT = D // P
IT = INNER // P
GH = 4
GROUPS = HEADS // GH
NG = BATCH * GROUPS
QT = SEQ // P
VW = HD + 1
JOBS = 12
HALF = INNER // 2
NHALF = 2 * JOBS
CLIP = 8.0
EPS = 1e-5
SCALE = HD ** -0.5
ROWS_MAX = 108
ROWS = 111


def build(nc, x, wproj, lnw, w_all, z_all, s_all, ident_in, identb_in, tri_in, behind_in, qrows, krows, out):
    stk = nc.dram_tensor("stk", [2, BATCH, P, KT, 3, SEQ], BF16).ap()
    vscr = nc.dram_tensor("vscr", [BATCH, QT, P, GROUPS, GH * VW], F32).ap()

    x_t = x.rearrange("b (t p) d -> (b t) p d", p=P)
    out_t = out.rearrange("b (t p) d -> (b t) p d", p=P)

    with ExitStack() as ctx:
        def sem(name):
            return ctx.enter_context(nc.semaphore(name))

        def sb_in(c):
            return lambda name, shape, dt: c.enter_context(nc.sbuf_tensor(name, shape, dt))

        sb = sb_in(ctx)
        bank = [ctx.enter_context(nc.psum_tensor(f"bank{n}", [P, 512], F32)) for n in range(4)]
        pair = [ctx.enter_context(nc.psum_tensor(f"pair{n}", [P, 2, 512], F32)) for n in range(2)]

        wo_hi = sb("wo_hi", [P, KT, D], F32R)
        wo_lo = sb("wo_lo", [P, KT, D], F32R)
        ident = sb("ident", [P, P], F32)
        identb = sb("identb", [P, P], BF16)
        xmean = sb("xmean", [P, TILES], F32)
        xrstd = sb("xrstd", [P, TILES], F32)

        sg0 = sb("sg0", [P, 512], F32)
        tri = sg0
        mx0 = sb("mx0", [P, GH, 4], F32)
        mx1 = sb("mx1", [P, 2, GH, 4], F32)
        s_sb = sb("s_sb", [P, 4, 512], F32)
        xin_c = sb("xin_c", [P, 4, D], F32)
        oin_v = sb("oin_v", [P, QT * GH * VW], F32)

        def as_slot(t, **sizes):
            flat = t[:, :, :].rearrange("p k s -> p (k s)").bitcast(BF16)
            return flat.rearrange("p (b j s) -> p b j s", j=GH, **sizes)
        qs, ks = [as_slot(s_sb, b=2)], [as_slot(xin_c, b=1)[:, 0]]
        vs = [oin_v[:, :].rearrange("p (t w) -> p t w", t=QT)]
        oin = oin_v[:, 0:D]

        with ExitStack() as ca:
            sa = sb_in(ca)
            raw_qkv = sa("raw_qkv", [P, KT, 3 * D], F32)
            raw_out = sa("raw_out", [P, KT, D], F32)
            wq_hi = sa("wq_hi", [P, KT, 3 * D], F32R)
            wq_lo = sa("wq_lo", [P, KT, 3 * D], F32R)
            lnb = sa("lnb", [P, 4, D], F32)
            xin = sa("xin", [P, 2, D], F32)
            xn = sa("xn", [P, D], F32)
            xt_hi = sa("xt_hi", [P, 2, KT, P], F32R)
            xt_lo = sa("xt_lo", [P, 2, KT, P], F32R)
            qk = sa("qk", [P, 2, D], F32)
            res = sa("res", [P, 2, D], F32)
            parts = [sa(f"parts{n}", [P, 2, KT, 3, 2 * P], BF16) for n in range(2)]
            vst = sa("vst", [P, 2, HEADS, VW], F32)
            st6x = sa("st6x", [P, 6], F32)
            st6q = sa("st6q", [P, 2, 6], F32)
            mvx = sa("mvx", [P, 2, 2], F32)
            mvq = sa("mvq", [P, 2, 2], F32)
            vex = sa("vex", [P, 3], F32)
            rsq = sa("rsq", [P, 2], F32)
            mhalf = sa("mhalf", [P, 1], F32)

        w_f = sb("w_f", [P, JOBS * INNER], F32)
        o_sb = sb("o_sb", [P, NG, QT, GH * HD], F32)
        with ExitStack() as cb:
            sbb = sb_in(cb)
            qs.append(sbb("qs1", [P, 2, GH, 512], BF16))
            ks.append(sbb("ks1", [P, GH, SEQ], BF16))
            vs.append(sbb("vs1", [P, QT, GH * VW], F32))
            pr = [sbb(f"pr{n}", [P, GH, 512], F32) for n in range(3)]
            ot = sbb("ot", [P, 512], F32)
            behind = sbb("behind", [P, P], BF16)
            zst = sbb("zst", [P, HALF], F32)
            sst = sbb("sst", [P, HALF], F32)
            dneg = sbb("dneg", [P, 16], F32)
            dres = sbb("dres", [P, 16], F32)
            d3 = sbb("d3", [P, 3, 16], BF16)
            dt_sb = [sbb(f"dt{n}", [48, P], BF16) for n in range(2)]
            rec = sbb("rec", [P, 2, 4, GH], F32)
        with ExitStack() as cc:
            sc = sb_in(cc)
            xc_hi = sc("xc_hi", [P, KT, 512], F32R)
            xc_lo = sc("xc_lo", [P, KT, 512], F32R)
            ws_hi = [sc(f"ws_hi{n}", [P, 3, 512], F32R) for n in range(2)]
            ws_lo = [sc(f"ws_lo{n}", [P, 3, 512], F32R) for n in range(2)]
            h_hi = [sc(f"h_hi{n}", [P, 512], F32R) for n in range(2)]
            h_lo = [sc(f"h_lo{n}", [P, 512], F32R) for n in range(2)]
            sg = [sg0, sc("sg1", [P, 512], F32)]
            xnc = sc("xnc", [P, 2, D], F32)

        passed = {kind: sem(f"passed_{kind}") for kind in ("pool", "dve", "pe", "sp")}

        def apart(eng, kind):
            eng.sem_inc(passed[kind], 1)

        stk_in = [[sem(f"stk_in{n}_{b}") for b in range(2)] for n in range(2)]
        LOADS = (16 * 15, 16 * 14)

        def load(sp, i, s, b):
            cols = slice(b * 512, (b + 1) * 512)
            p0 = (i % 2) * 64
            for r, both in enumerate(((0, 0), (1, 0), (2, 0), (0, 1), (1, 1), (0, 2))):
                rows = slice(r * HD, (r + 1) * HD)
                src = stk[:, bass.ds(i // GROUPS, 1), bass.ds(p0, 64), bass.ds((i % GROUPS) // 2, 1), :, :]
                for a, dst in enumerate((qs[s][rows, b, :, :], ks[s][rows, :, cols])):
                    part = src[a].rearrange("a (j c) k w s -> w c (a j) (k s)", j=GH)[both[a]]
                    sp.dma_start(dst, part[:, :, cols]).then_inc(stk_in[s][b], 16)
            g = i % GROUPS
            sp.dma_start(qs[s][96:ROWS_MAX, b, :, :], qrows[bass.ds(g, 1), :, :, cols].rearrange("a p j s -> (a p) j s"))\
              .then_inc(stk_in[s][b], 16)
            sp.dma_start(ks[s][96:ROWS, :, cols], krows[bass.ds(g, 1), :, :, cols].rearrange("a p j s -> (a p) j s"))\
              .then_inc(stk_in[s][b], 16)
            if b == 0:
                sp.dma_start(vs[s][:, :, :], vscr[i // GROUPS, :, :, g, :].rearrange("t p w -> p t w"))\
                  .then_inc(stk_in[s][b], 16)

        m_full, m_free, mx1_done, tri_done = sem("m_full"), sem("m_free"), sem("mx1_done"), sem("tri_done")
        b_m, b_o = bank[0:3], bank[3]
        STEPS = [(qb, kt, max(0, (kt - 4 * qb) * P)) for qb in (1, 0) for kt in range(4 * qb + 4)]
        NSTEP = len(STEPS)
        FIRST = 8
        diag = [kt >= 4 * qb for qb, kt, _ in STEPS]

        def pieces(tiles):
            return [(qt, j, k0, min(512, (qt + 1) * P - k0))
                    for qt in tiles for j in range(GH) for k0 in range(0, (qt + 1) * P, 512)]
        EARLY = sorted(pieces(range(4, 8)), key=lambda pc: -pc[2])
        LATE = pieces(range(4))
        HEAD = 8
        LATER_KEYS = len(EARLY) // 2
        PLACES = 3 * NSTEP
        OWN_END = 8
        LOW_AT = 15
        EARLY_END = 28
        TAIL = 6
        BEFORE = 4
        D0_AT, D1_AT, O1_AT = 5, 10, 9
        JOB_AT = 6

        def spread(lot, lo, hi):
            width = [w for e in range(NSTEP) for w in (512 - STEPS[e][2], 512 - STEPS[e][2], 512 - STEPS[e - 1][2])]
            total, work = sum(width[lo:hi]), sum(pc[3] + 60 for pc in lot)
            out, at, passed = {h: [] for h in range(PLACES)}, 0, 0
            for h in range(lo, hi):
                passed += width[h]
                while at < len(lot) and (h == hi - 1 or sum(pc[3] + 60 for pc in lot[:at]) < work * passed / total):
                    out[h].append(lot[at])
                    at += 1
            return out
        parts_of_plan = (spread(LATE[HEAD:], 0, OWN_END), spread(EARLY[:LATER_KEYS], OWN_END - 1, LOW_AT),
                         spread(EARLY[LATER_KEYS:], LOW_AT, EARLY_END), spread(LATE[:HEAD - TAIL], EARLY_END, PLACES))
        plan = {h: sum((part[h] for part in parts_of_plan), []) for h in range(PLACES)}
        plan[3 * D0_AT + 2].append("D0")
        plan[3 * O1_AT + 2].append("O1")
        tail = LATE[HEAD - TAIL:HEAD] + ["O0"]
        own = [x for h in range(PLACES) for x in plan[h] if x in LATE[HEAD:] or isinstance(x, str)] + ["O0"]
        order = [x for h in range(PLACES) for x in plan[h]] + tail
        RING = len(order)
        assert RING % 3 == 0
        HEAD_ORDER = EARLY + LATE[:HEAD]
        PREP = len(HEAD_ORDER)
        number = ({x: n for n, x in enumerate(order)}, {x: n for n, x in enumerate(own)})

        def at(x, last):
            return number[last is True][x]

        def ring_bank(x, last):
            return b_m[(PREP + at(x, last)) % 3]

        def base(i):
            return PREP + RING * i

        def take(dve, pc, b, n):
            qt, j, k0, w = pc
            src = b[:, 0:w]
            dst = mx0[:, j, qt:qt + 1] if qt < 4 else mx1[:, k0 // 512, j, qt - 4:qt - 3]
            dve.wait_ge(m_full, n + 1)
            if k0 + w == (qt + 1) * P:
                apart(dve, "dve")
                dve.tensor_tensor_reduce(out=src, in0=src, in1=tri[:, 512 - w:512], scale=1.0,
                                         scalar=-3.0e38, op0=ALU.add, op1=ALU.max, accum_out=dst).then_inc(m_free, 1)
            else:
                dve.tensor_reduce(dst, src, AX.X, ALU.max).then_inc(m_free, 1)

        def score(pe, s, pc, b, n):
            qt, j, k0, w = pc
            if not (isinstance(n, int) and n < 3):
                pe.wait_ge(m_free, n - 2)
            pe.matmul(b[:, 0:w], qs[s][0:ROWS_MAX, qt // 4, j, (qt % 4) * P:(qt % 4 + 1) * P],
                      ks[s][0:ROWS_MAX, j, k0:k0 + w], start=True, stop=True).then_inc(m_full, 1)

        def over_halves(dve, n):
            dve.wait_ge(m_free, n)
            dve.tensor_tensor(mx1[:, 0, :, :], mx1[:, 0, :, :], mx1[:, 1, :, :], ALU.max).then_inc(mx1_done, 1)

        raw_in, x_in = [sem(f"raw_in{kt}") for kt in range(KT)], [sem(f"x_in{u}") for u in range(2)]
        cst_in, lnw_in, wo_in = sem("cst_in"), sem("lnw_in"), sem("wo_in")
        wo_hi_done, wo_lo_done = sem("wo_hi_done"), sem("wo_lo_done")
        setup_done = sem("setup_done")
        whi_done, wlo_done = sem("whi_done"), sem("wlo_done")
        x_stat, x_mv, x_var, x_rstd, xn_done = sem("x_stat"), sem("x_mv"), sem("x_var"), sem("x_rstd"), sem("xn_done")
        xt_ps, xhi_done, xlo_done = sem("xt_ps"), sem("xhi_done"), sem("xlo_done")
        proj_v, proj_q, proj_k = sem("proj_v"), sem("proj_q"), sem("proj_k")
        v_copy, v_clip, v_out = sem("v_copy"), sem("v_clip"), [sem(f"v_out{u}") for u in range(2)]
        qk_clip, qk_stat, qk_mv, qk_mid = sem("qk_clip"), sem("qk_stat"), sem("qk_mv"), sem("qk_mid")
        qk_var, qk_rstd, qk_ln = sem("qk_var"), sem("qk_rstd"), sem("qk_ln")
        qk_ps, part_h, part_r, part_m, part_l, part_out = (
            sem("qk_ps"), sem("part_h"), sem("part_r"), sem("part_m"), sem("part_l"), [sem(f"part_out{n}") for n in range(2)])

        LAST = TILES // 2 - 1
        W_COLS = slice(2 * D, 3 * D), slice(0, 2 * D)
        FILL_A, FILL_B = 2, 5
        b_xt, b_v, b_q, b_k = (bank[n] for n in range(4))
        b_t = [pair[0][:, n, :] for n in range(2)]

        def tile_pairs(eng, body):
            for s in range(2):
                body(s, s, 0, s == 0, False)
            with eng.Fori(1, LAST // 2) as q:
                for s in range(2):
                    body(2 * q + s, s, q, False, False)
            for s in range(2):
                body(LAST - 1 + s, s, LAST // 2, False, s == 1)

        def wo_parts(t):
            return {2: (0, 1), 3: (2, 3)}.get(t, ()) if isinstance(t, int) else ()

        with nc.Block() as block:
            @block.sync
            def _(sp):
                sp.dma_start(xin[:, 0, :], x_t[0]).then_inc(x_in[0], 16)
                for kt in range(KT):
                    sp.dma_start(raw_qkv[:, kt, :], wproj[kt, :, 0:3 * D]).then_inc(raw_in[kt], 16)
                    if kt == 0:
                        sp.dma_start(ident[:, :], ident_in).then_inc(cst_in, 16)
                        sp.dma_start(identb[:, :], identb_in).then_inc(cst_in, 16)
                        sp.dma_start(xin[:, 1, :], x_t[1]).then_inc(x_in[1], 16)
                sp.dma_start(lnb[:, :, :], lnw.rearrange("(a n) d -> a n d", a=1).to_broadcast([P, 4, D]))\
                  .then_inc(lnw_in, 16)

                def body(c, s, q, first, last):
                    if last:
                        for n in range(2):
                            sp.wait_ge(v_out[n], 8 * QT)
                            sp.wait_ge(part_out[n], 8 * QT)
                        for b in (1, 0):
                            load(sp, 0, 0, b)
                    for u in range(2):
                        t = 2 * c + u
                        if not last:
                            sp.wait_ge(xn_done, t + 1)
                            sp.dma_start(xin[:, u, :], x_t[t + 2]).then_inc(x_in[u], 16)
                        if first and u == 1:
                            sp.dma_start(tri[:, :], tri_in).then_inc(tri_done, 16)
                            sp.dma_start(raw_out[:, :, :], wproj[:, :, 3 * D:].rearrange("k p c -> p k c"))\
                              .then_inc(wo_in, 16)
                        sp.wait_ge(v_clip, t + 1)
                        sp.dma_start(vscr[t // QT, t % QT], vst[:, u, :, :].rearrange("p (g h) w -> p g (h w)", g=GROUPS))\
                          .then_inc(v_out[u], 16)
                tile_pairs(sp, body)
                for n in range(2):
                    sp.wait_ge(v_out[n], 8 * TILES)
                    sp.wait_ge(part_out[n], 16 * (LAST + 1))

            @block.gpsimd
            def _(pool):
                pool.memset(mhalf[:, :], -0.5).then_inc(setup_done, 1)
                pool.memset(vst[:, :, :, :], 1.0).then_inc(setup_done, 1)
                pool.wait_ge(setup_done, 2)

                def x_rs(t, u):
                    pool.wait_ge(x_mv, t + 1)
                    apart(pool, "pool")
                    pool.tensor_scalar(vex[:, 0:1], mvx[:, u, 1:2], EPS, None, ALU.add).then_inc(x_var, 1)
                    pool.wait_ge(x_var, t + 1)
                    apart(pool, "pool")
                    pool.tensor_tensor(xrstd[:, bass.ds(t, 1)], vex[:, 0:1], mhalf[:, :], ALU.pow).then_inc(x_rstd, 1)

                def qk_rs(t, a):
                    pool.wait_ge(qk_mv, 2 * t + a + 1)
                    apart(pool, "pool")
                    pool.tensor_scalar(vex[:, 1 + a:2 + a], mvq[:, a, 1:2], EPS, None, ALU.add).then_inc(qk_var, 1)
                    pool.wait_ge(qk_var, 2 * t + a + 1)
                    pool.tensor_tensor(rsq[:, a:a + 1], vex[:, 1 + a:2 + a], mhalf[:, :], ALU.pow).then_inc(qk_rstd, 1)

                def low(t, u, s):
                    for a in range(2):
                        pool.wait_ge(part_m, 2 * t + a + 1)
                        pool.tensor_tensor(parts[s][:, a, :, 2, u * P:(u + 1) * P],
                                           res[:, a, :].rearrange("p (k s) -> p k s", k=KT),
                                           parts[s][:, a, :, 1, u * P:(u + 1) * P], ALU.subtract).then_inc(part_l, 1)
                def clip_v(t, u):
                    pool.wait_ge(v_copy, t + 1)
                    apart(pool, "pool")
                    v = vst[:, u, :, 0:HD]
                    pool.tensor_scalar(v, v, CLIP, -CLIP, ALU.min, ALU.max).then_inc(v_clip, 1)

                x_rs(0, 0)
                x_rs(1, 1)

                def body(c, s, q, first, last):
                    for u in range(2):
                        t = 2 * c + u
                        if not (first and u == 0):
                            qk_rs(t - 1, 1)
                        if not last:
                            x_rs(t + 2, u)
                        clip_v(t, u)
                        if not (first and u == 0):
                            low(t - 1, 1 - u, s if u == 1 else 1 - s)
                        qk_rs(t, 0)
                        for kt in wo_parts(t):
                            pool.wait_ge(wo_hi_done, kt + 1)
                            pool.tensor_tensor(wo_lo[:, kt, :], raw_out[:, kt, :], wo_hi[:, kt, :].bitcast(F32),
                                               ALU.subtract).then_inc(wo_lo_done, 1)
                tile_pairs(pool, body)
                qk_rs(TILES - 1, 1)
                low(TILES - 1, 1, 1)

            @block.scalar
            def _(act):
                def x_hi(t, u):
                    act.wait_ge(xt_ps, t + 1)
                    if not (isinstance(t, int) and t < 2):
                        act.wait_ge(proj_k, t - 1)
                    act.activation(xt_hi[:, u, :, :].rearrange("p k s -> p (k s)"), b_xt[:, :], ACT.Copy)\
                       .then_inc(xhi_done, 1)

                def copy_v(t, u, c):
                    act.wait_ge(proj_v, t + 1)
                    if not (isinstance(t, int) and t < 2):
                        act.wait_ge(v_out[u], 16 * c)
                    act.activation(vst[:, u, :, 0:HD], b_v[:, :].rearrange("p (h d) -> p h d", h=HEADS), ACT.Copy)\
                       .then_inc(v_copy, 1)

                def high(t, u, a, s):
                    act.wait_ge(qk_ps, 2 * t + a + 1)
                    act.activation(parts[s][:, a, :, 0, u * P:(u + 1) * P],
                                   b_t[a].rearrange("p (k s) -> p k s", k=KT), ACT.Copy).then_inc(part_h, 1)

                def mid(t, u, a, s):
                    act.wait_ge(part_r, 2 * t + a + 1)
                    act.activation(parts[s][:, a, :, 1, u * P:(u + 1) * P],
                                   res[:, a, :].rearrange("p (k s) -> p k s", k=KT), ACT.Copy).then_inc(part_m, 1)

                def split(t, u, s, stored):
                    if stored is not None:
                        act.wait_ge(part_out[s], stored)
                    high(t, u, 0, s)
                    high(t, u, 1, s)
                    mid(t, u, 0, s)
                    mid(t, u, 1, s)
                def store_parts(c, s, need):
                    act.wait_ge(part_l, need)
                    for a in range(2):
                        dst = stk[a, bass.ds(c // 4, 1), :, :, :, bass.ds((c % 4) * 2 * P, 2 * P)]
                        act.dma_start(dst.rearrange("a p k w s -> (a p) (k w) s"),
                                     parts[s][:, a, :, :, :].rearrange("p k w s -> p (k w) s")).then_inc(part_out[s], 16)

                for kt in range(KT):
                    act.wait_ge(raw_in[kt], 16)
                    for cols in W_COLS:
                        act.activation(wq_hi[:, kt, cols], raw_qkv[:, kt, cols], ACT.Copy).then_inc(whi_done, 1)
                    if kt == 1:
                        x_hi(0, 0)

                def body(c, s, q, first, last):
                    for u in range(2):
                        t = 2 * c + u
                        copy_v(t, u, c)
                        if not (last and u == 1):
                            x_hi(t + 1, 1 - u)
                        if u == 1 and not first:
                            store_parts(c - 1, 1 - s, 4 * c)
                        if not (first and u == 0):
                            reused = u == 1 and not (isinstance(q, int) and q == 0)
                            split(t - 1, 1 - u, s if u == 1 else 1 - s, 16 * 2 * q if reused else None)
                        for kt in wo_parts(t):
                            act.wait_ge(wo_in, 16)
                            act.activation(wo_hi[:, kt, :], raw_out[:, kt, :], ACT.Copy).then_inc(wo_hi_done, 1)
                tile_pairs(act, body)
                split(TILES - 1, 1, 1, None)
                store_parts(LAST, 1, 2 * TILES)

            @block.vector
            def _(dve):
                def x_stats(t, u, c):
                    dve.wait_ge(x_in[u], 16 * c + 16)
                    dve.bn_stats(st6x[:, :], xin[:, u, :]).then_inc(x_stat, 1)

                def x_aggr(t, u):
                    dve.wait_ge(x_stat, t + 1)
                    apart(dve, "dve")
                    dve.bn_aggr(mvx[:, u, :], st6x[:, :]).then_inc(x_mv, 1)

                def keep_mean(t, u):
                    dve.wait_ge(x_mv, t + 1)
                    apart(dve, "dve")
                    dve.tensor_copy(xmean[:, bass.ds(t, 1)], mvx[:, u, 0:1])

                def x_norm(t, u):
                    dve.wait_ge(x_rstd, t + 1)
                    if not (isinstance(t, int) and t < 1):
                        dve.wait_ge(xt_ps, t)
                    dve.tensor_scalar(xn[:, :], xin[:, u, :], mvx[:, u, 0:1], xrstd[:, bass.ds(t, 1)],
                                      ALU.subtract, ALU.mult).then_inc(xn_done, 1)

                def x_lo(t, u):
                    dve.wait_ge(xhi_done, t + 1)
                    dve.tensor_tensor(xt_lo[:, u, :, :].rearrange("p k s -> p (k s)"), b_xt[:, :],
                                      xt_hi[:, u, :, :].rearrange("p k s -> p (k s)").bitcast(F32), ALU.subtract)\
                       .then_inc(xlo_done, 1)

                def clip(t, a):
                    dve.wait_ge((proj_q, proj_k)[a], t + 1)
                    if not (isinstance(t, int) and t < 1):
                        dve.wait_ge(qk_ps, 2 * t - 1 + a)
                    dve.tensor_scalar(qk[:, a, :], (b_q, b_k)[a][:, :], CLIP, -CLIP, ALU.min, ALU.max).then_inc(qk_clip, 1)

                def stats(t, a):
                    dve.wait_ge(qk_clip, 2 * t + a + 1)
                    dve.bn_stats(st6q[:, a, :], qk[:, a, :]).then_inc(qk_stat, 1)

                def aggr(t, a):
                    dve.wait_ge(qk_stat, 2 * t + a + 1)
                    apart(dve, "dve")
                    dve.bn_aggr(mvq[:, a, :], st6q[:, a, :]).then_inc(qk_mv, 1)

                def center(t, a):
                    dve.wait_ge(qk_mv, 2 * t + a + 1)
                    dve.scalar_tensor_tensor(out=qk[:, a, :], in0=qk[:, a, :], scalar=mvq[:, a, 0:1],
                                             in1=lnb[:, 2 * a, :], op0=ALU.subtract, op1=ALU.mult).then_inc(qk_mid, 1)

                def rescale(t, a):
                    dve.wait_ge(qk_mid, 2 * t + a + 1)
                    dve.wait_ge(qk_rstd, 2 * t + a + 1)
                    dve.scalar_tensor_tensor(out=qk[:, a, :], in0=qk[:, a, :], scalar=rsq[:, a:a + 1],
                                             in1=lnb[:, 2 * a + 1, :], op0=ALU.mult, op1=ALU.add).then_inc(qk_ln, 1)

                def residual(t, u, a, s):
                    dve.wait_ge(part_h, 2 * t + a + 1)
                    if not (isinstance(t, int) and t < 1):
                        dve.wait_ge(part_l, 2 * t - 1 + a)
                    dve.tensor_tensor(res[:, a, :].rearrange("p (k s) -> p k s", k=KT),
                                      b_t[a].rearrange("p (k s) -> p k s", k=KT),
                                      parts[s][:, a, :, 0, u * P:(u + 1) * P], ALU.subtract).then_inc(part_r, 1)

                x_stats(0, 0, 0)
                x_aggr(0, 0)
                keep_mean(0, 0)
                x_norm(0, 0)
                for kt in range(KT):
                    for n, cols in enumerate(W_COLS):
                        dve.wait_ge(whi_done, 2 * kt + n + 1)
                        dve.tensor_tensor(wq_lo[:, kt, cols], raw_qkv[:, kt, cols], wq_hi[:, kt, cols].bitcast(F32), ALU.subtract)\
                           .then_inc(wlo_done, 1)
                    if kt == 0:
                        x_stats(1, 1, 0)
                        x_aggr(1, 1)
                        keep_mean(1, 1)
                    if kt == 1:
                        x_lo(0, 0)
                x_norm(1, 1)
                dve.wait_ge(setup_done, 2)
                dve.wait_ge(lnw_in, 16)

                def body(c, s, q, first, last):
                    for u in range(2):
                        t = 2 * c + u
                        prev = not (first and u == 0)
                        if prev:
                            clip(t - 1, 1)
                        if not last:
                            x_stats(t + 2, u, c + 1)
                        if prev:
                            stats(t - 1, 1)
                            center(t - 1, 0)
                            aggr(t - 1, 1)
                        if not last:
                            x_aggr(t + 2, u)
                        if prev:
                            center(t - 1, 1)
                            rescale(t - 1, 0)
                        if not last:
                            keep_mean(t + 2, u)
                        if prev:
                            rescale(t - 1, 1)
                        if not (last and u == 1):
                            x_lo(t + 1, 1 - u)
                        clip(t, 0)
                        if not last:
                            x_norm(t + 2, u)
                        stats(t, 0)
                        if prev:
                            residual(t - 1, 1 - u, 0, s if u == 1 else 1 - s)
                        aggr(t, 0)
                        if prev:
                            residual(t - 1, 1 - u, 1, s if u == 1 else 1 - s)
                tile_pairs(dve, body)
                t = TILES - 1
                dve.wait_ge(tri_done, 16)
                clip(t, 1)
                stats(t, 1)
                center(t, 0)
                aggr(t, 1)
                for n in range(FILL_A):
                    take(dve, EARLY[n], b_m[n % 3], n)
                center(t, 1)
                for a in range(2):
                    rescale(t, a)
                for n in range(FILL_A, FILL_B):
                    take(dve, EARLY[n], b_m[n % 3], n)
                for a in range(2):
                    residual(t, 1, a, 1)
                for n in range(FILL_B, len(EARLY)):
                    take(dve, EARLY[n], b_m[n % 3], n)
                over_halves(dve, len(EARLY))

            @block.tensor
            def _(pe):
                def x_trans(t):
                    pe.wait_ge(xn_done, t + 1)
                    if not (isinstance(t, int) and t < 1):
                        pe.wait_ge(xlo_done, t)
                    for kt in range(KT):
                        mm = pe.transpose(b_xt[:, kt * P:(kt + 1) * P], xn[:, kt * P:(kt + 1) * P], ident[:, :])
                    mm.then_inc(xt_ps, 1)

                def project(t, u, n, b, done, free):
                    pe.wait_ge(xlo_done, t + 1)
                    if not (isinstance(t, int) and t < 1):
                        pe.wait_ge(*free)
                    cols = slice(n * D, (n + 1) * D)
                    for kt in range(KT):
                        if isinstance(t, int) and t < 1:
                            pe.wait_ge(wlo_done, 2 * kt + (1 if n == 2 else 2))
                        for i, (l, r) in enumerate(((xt_lo, wq_hi), (xt_hi, wq_lo), (xt_hi, wq_hi))):
                            mm = pe.matmul(b[:, :], l[:, u, kt, :], r[:, kt, cols],
                                           start=(kt == 0 and i == 0), stop=(kt == KT - 1 and i == 2))
                    mm.then_inc(done, 1)

                def qk_trans(t):
                    for a in range(2):
                        pe.wait_ge(qk_ln, 2 * t + a + 1)
                        if not (isinstance(t, int) and t < 1):
                            pe.wait_ge(part_r, 2 * t - 1 + a)
                        for kt in range(KT):
                            mm = pe.transpose(b_t[a][:, kt * P:(kt + 1) * P], qk[:, a, kt * P:(kt + 1) * P], ident[:, :])
                        mm.then_inc(qk_ps, 1)
                pe.wait_ge(cst_in, 32)
                x_trans(0)

                def body(c, s, q, first, last):
                    for u in range(2):
                        t = 2 * c + u
                        project(t, u, 2, b_v, proj_v, (v_copy, t))
                        if not (last and u == 1):
                            x_trans(t + 1)
                        project(t, u, 0, b_q, proj_q, (qk_clip, 2 * t - 1))
                        if not (first and u == 0):
                            qk_trans(t - 1)
                        project(t, u, 1, b_k, proj_k, (qk_clip, 2 * t))
                tile_pairs(pe, body)
                for n, pc in enumerate(EARLY):
                    if n == 0:
                        pe.wait_ge(stk_in[0][1], LOADS[1])
                    if n == LATER_KEYS:
                        pe.wait_ge(stk_in[0][0], LOADS[0])
                    if n < 3:
                        pe.wait_ge(*((xlo_done, TILES), (v_copy, TILES), (qk_clip, 2 * TILES - 1))[n])
                    if n == FILL_B:
                        qk_trans(TILES - 1)
                    score(pe, 0, pc, b_m[n % 3], n)

        xc_in, xuse_d, xuse_p = [sem(f"xc_in{n}") for n in range(4)], sem("xuse_d"), sem("xuse_p")

        def load_x(sp, b, u):
            sp.dma_start(xin_c[:, u, :], x_t[4 * b + u]).then_inc(xc_in[u], 16)

        mask_in = sem("mask_in")
        s_full = [sem(f"s_full{n}") for n in range(2)]
        exp_done, pv_done = sem("exp_done"), sem("pv_done")
        d_chain, d_copied, d0_in, d1_in = sem("d_chain"), sem("d_copied"), sem("d0_in"), sem("d1_in")
        ot_done, rec_done, o_clear = sem("ot_done"), sem("rec_done"), sem("o_clear")
        z_in, z_conv, z_sub, z_mul = sem("z_in"), sem("z_conv"), sem("z_sub"), sem("z_mul")

        USES = (NSTEP + 1, NSTEP)
        D1_USE = D1_AT + 1
        EXTRA = 1
        PV0 = 3

        def full(i, e, p, last):
            return USES[p] * i + e + 1 + (1 + (e > D1_AT and not last) if p == 0 else 0)

        def full_d1(i):
            return USES[0] * i + D1_USE + 2

        def groups(eng, body):
            with eng.Fori(0, NG // 2 - 1) as ip:
                for s in range(2):
                    body(2 * ip + s, s, ip, None)
            for s in range(2):
                body(NG - 2 + s, s, NG // 2 - 1, s == 1)

        with nc.Block() as block:
            @block.sync
            def _(sp):
                def half_job(jj):
                    if not (isinstance(jj, int) and jj == 0):
                        sp.wait_ge(z_mul, jj)
                    sp.dma_start(zst[:, :].bitcast(I32), z_all[bass.ds(jj, 1), :].to_broadcast([P, HALF])).then_inc(z_in, 16)
                    sp.dma_start(sst[:, :], s_all[bass.ds(jj, 1), :].to_broadcast([P, HALF])).then_inc(z_in, 16)
                    sp.dma_start(w_f[:, bass.ds(jj * HALF, HALF)].bitcast(I32), w_all[bass.ds(jj, 1)].rearrange("a p c -> (a p) c"))\
                      .then_inc(z_in, 16)

                sp.dma_start(behind[:, :], behind_in).then_inc(mask_in, 16)
                for b in (1, 0):
                    load(sp, 1, 1, b)
                half_job(0)

                def body(i, s, ip, last):
                    if s == 1:
                        half_job(3 * ip + 2)
                    if not last:
                        half_job(3 * ip + (1, 3)[s])
                    else:
                        sp.wait_ge(pv_done, PV0 + NSTEP * i)
                        for u in range(4):
                            load_x(sp, 0, u)
                    if last is None:
                        sp.wait_ge(pv_done, PV0 + NSTEP * i + FIRST)
                        apart(sp, "sp")
                        load(sp, i + 2, s, 1)
                        sp.wait_ge(pv_done, PV0 + NSTEP * i + NSTEP)
                        apart(sp, "sp")
                        load(sp, i + 2, s, 0)
                groups(sp, body)

            @block.gpsimd
            def _(pool):
                pool.sem_inc(ot_done, EXTRA)
                pool.sem_inc(pv_done, PV0)

                def chain(mx, n):
                    apart(pool, "pool")
                    pool.tensor_scalar(dneg[:, :], mx.rearrange("p j t -> p (j t)"), -1.0, None, ALU.mult).then_inc(d_chain, 1)
                    pool.wait_ge(d_chain, 5 * n + 1)
                    apart(pool, "pool")
                    pool.tensor_copy(d3[:, 0, :], dneg[:, :]).then_inc(d_chain, 1)
                    pool.wait_ge(d_chain, 5 * n + 2)
                    pool.tensor_tensor(dres[:, :], dneg[:, :], d3[:, 0, :], ALU.subtract).then_inc(d_chain, 1)
                    pool.wait_ge(d_chain, 5 * n + 3)
                    apart(pool, "pool")
                    pool.tensor_copy(d3[:, 1, :], dres[:, :]).then_inc(d_chain, 1)
                    pool.wait_ge(d_chain, 5 * n + 4)
                    pool.tensor_tensor(d3[:, 2, :], dres[:, :], d3[:, 1, :], ALU.subtract).then_inc(d_chain, 1)

                def job(jj):
                    w = w_f[:, bass.ds(jj * HALF, HALF)]
                    pool.wait_ge(z_conv, jj + 1)
                    apart(pool, "pool")
                    pool.tensor_tensor(w, w, zst[:, :], ALU.subtract).then_inc(z_sub, 1)
                    pool.wait_ge(z_sub, jj + 1)
                    apart(pool, "pool")
                    pool.tensor_tensor(w, w, sst[:, :], ALU.mult).then_inc(z_mul, 1)

                pool.wait_ge(mx1_done, 1)
                chain(mx1[:, 0, :, :], 0)

                def body(i, s, ip, last):
                    pool.wait_ge(m_free, base(i) + at(LATE[-1], last) + 1)
                    pool.wait_ge(s_full[0], USES[0] * i + 1)
                    chain(mx0[:, :, :], 2 * i + 1)
                    job(3 * ip + (0, 2)[s])
                    if not last:
                        pool.wait_ge(mx1_done, i + 2)
                        pool.wait_ge(m_full, base(i) + at("D0", last) + 1)
                        chain(mx1[:, 0, :, :], 2 * i + 2)
                    if s == 0:
                        job(3 * ip + 1)
                groups(pool, body)

            @block.scalar
            def _(act):
                def send_d(s, b, done):
                    act.dma_start(qs[s][ROWS_MAX:ROWS, b, :, :].rearrange("a j (t c) -> a (j t) c", c=P), dt_sb[b][:, :])\
                       .then_inc(done, 16)

                def send_d1(s, count, n):
                    act.wait_ge(s_full[0], count)
                    act.activation(dt_sb[1][:, :], pair[0][0:48, 0, 0:P // 2].bitcast(BF16), ACT.Copy).then_inc(d_copied, 1)
                    act.wait_ge(d_copied, n)
                    send_d(s, 1, d1_in)

                def exps(i, e, p, last):
                    w = 512 - STEPS[e][2]
                    act.wait_ge(s_full[p], full(i, e, p, last))
                    act.wait_ge(pv_done, NSTEP * i + e + 1)
                    act.activation(pr[e % 3][:, 2 * p:2 * p + 2, 0:w], pair[p][:, :, 0:w], ACT.Exp, scale=SCALE)\
                       .then_inc(exp_done, 1)

                def copy_o(i, k):
                    act.wait_ge(pv_done, PV0 + NSTEP * i + (FIRST, NSTEP)[k])
                    act.activation(ot[:, :], b_o[:, :], ACT.Copy).then_inc(ot_done, 1)

                def convert(jj):
                    w = w_f[:, bass.ds(jj * HALF, HALF)]
                    act.wait_ge(z_in, 48 * jj + 48)
                    act.activation(w, w.bitcast(I32), ACT.Copy)
                    act.activation(zst[:, :], zst[:, :].bitcast(I32), ACT.Copy).then_inc(z_conv, 1)

                send_d1(0, 1, 1)

                def body(i, s, ip, last):
                    for e in range(NSTEP):
                        if e == JOB_AT:
                            convert(3 * ip + (0, 2)[s])
                        if e == D0_AT + 2:
                            act.wait_ge(m_free, base(i) + at("D0", last) + 1)
                            send_d(s, 0, d0_in)
                        if e == D1_AT + 1 and not last:
                            send_d1(1 - s, full_d1(i), i + 2)
                        if e == FIRST + 1:
                            copy_o(i, 0)
                        exps(i, e, 0, last)
                        exps(i, e, 1, last)
                    if D1_AT == NSTEP - 1 and not last:
                        send_d1(1 - s, full_d1(i), i + 2)
                    copy_o(i, 1)
                    if s == 0:
                        convert(3 * ip + 1)
                groups(act, body)

            @block.vector
            def _(dve):
                def normalise(i, k, last):
                    work, qb = ("O1", "O0")[k], 1 - k
                    dve.wait_ge(m_full, base(i) + at(work, last) + 1)
                    src = ring_bank(work, last)[:, :].rearrange("p (t j w) -> p t j w", t=4, j=GH)
                    dve.reciprocal(rec[:, k, :, :], src[:, :, :, HD]).then_inc(rec_done, 1)
                    dve.wait_ge(rec_done, 2 * i + k + 1)
                    dst = o_sb[:, bass.ds(i, 1), 4 * qb:4 * qb + 4, :].rearrange("p a t (j d) -> p (a t) j d", j=GH)
                    dve.tensor_tensor(dst, src[:, :, :, 0:HD], rec[:, k, :, :].unsqueeze(3).to_broadcast([P, 4, GH, HD]),
                                      ALU.mult).then_inc(m_free, 1)

                def ring(i, work, last=None):
                    for x in work:
                        if x == "D0":
                            dve.wait_ge(m_full, base(i) + at(x, last) + 1)
                            apart(dve, "dve")
                            dve.tensor_copy(dt_sb[0][:, :], ring_bank(x, last)[0:48, 0:P // 2].bitcast(BF16)).then_inc(m_free, 1)
                        elif isinstance(x, str):
                            normalise(i, int(x == "O0"), last)
                        elif x in LATE[HEAD:] or not last:
                            if x == EARLY[0]:
                                dve.wait_ge(d_chain, 10 * i + 1)
                            if x == LATE[0]:
                                dve.wait_ge(d_chain, 10 * i + 6)
                            take(dve, x, ring_bank(x, last), base(i) + at(x, last))
                            if x == EARLY[-1]:
                                over_halves(dve, base(i) + at(x, last) + 1)

                dve.memset(b_o[:, :], 0.0).then_inc(o_clear, 1)
                for n in range(len(EARLY), PREP):
                    take(dve, HEAD_ORDER[n], b_m[n % 3], n)

                def body(i, s, ip, last):
                    for h in range(PLACES):
                        ring(i, plan[h], last)
                    ring(i, tail, last)
                groups(dve, body)

            @block.tensor
            def _(pe):
                def ring(i, s, work, last=None):
                    for x in work:
                        if isinstance(x, str):
                            pe.wait_ge(m_free, base(i) + at(x, last) - 2)
                            if x == "D0":
                                trans_d(2 * i + 1, ring_bank(x, last), m_full)
                            else:
                                trans_o(i, int(x == "O0"), ring_bank(x, last))
                        elif x in LATE[HEAD:]:
                            score(pe, s, x, ring_bank(x, last), base(i) + at(x, last))
                        elif not last:
                            score(pe, 1 - s, x, ring_bank(x, last), base(i) + at(x, last))

                def trans_d(n, to, done):
                    pe.wait_ge(d_chain, 5 * n + 5)
                    apart(pe, "pe")
                    pe.transpose(to[0:48, 0:P // 2].bitcast(BF16), d3[:, :, :].rearrange("p a b -> p (a b)"), identb[:, :])\
                      .then_inc(done, 1)

                def slot0_free(i, e, last):
                    if e == D1_AT + 1 and not last:
                        pe.wait_ge(d_copied, i + 2)
                    elif e > 0:
                        pe.wait_ge(exp_done, 2 * NSTEP * i + 2 * e - 1)

                def second(i, s, e, p):
                    qb, kt, c0 = STEPS[e]
                    for jj in range(2):
                        j = 2 * p + jj
                        mm = pe.matmul(pair[p][:, jj, 0:512 - c0], ks[s][0:ROWS, j, kt * P:(kt + 1) * P],
                                       qs[s][0:ROWS, qb, j, c0:512], start=True, stop=not diag[e])
                    if diag[e]:
                        for jj in range(2):
                            mm = pe.matmul(pair[p][:, jj, 0:P], identb[:, :], behind[:, :], start=False, stop=True)
                    mm.then_inc(s_full[p], 1)

                def pv(i, s, e):
                    qb, kt, c0 = STEPS[e]
                    pe.wait_ge(exp_done, 2 * NSTEP * i + 2 * e + 2)
                    if kt == 0:
                        pe.wait_ge(ot_done, EXTRA + 2 * i + 1 - qb)
                    for j in range(GH):
                        mm = pe.matmul(b_o[32 * j:32 * j + VW, c0:512], vs[s][:, kt, j * VW:(j + 1) * VW],
                                       pr[e % 3][:, j, 0:512 - c0], start=(kt == 0), stop=(kt == 4 * qb + 3),
                                       tile_position=(0, 32 * j))
                    mm.then_inc(pv_done, 1)

                def trans_o(i, k, to):
                    pe.wait_ge(ot_done, EXTRA + 2 * i + k + 1)
                    for t in range(4):
                        mm = pe.transpose(to[:, t * P:(t + 1) * P], ot[:, t * P:(t + 1) * P], ident[:, :])
                    mm.then_inc(m_full, 1)

                for n in range(len(EARLY), PREP):
                    score(pe, 0, HEAD_ORDER[n], b_m[n % 3], n)
                trans_d(0, pair[0][:, 0, :], s_full[0])
                pe.wait_ge(o_clear, 1)
                pe.wait_ge(mask_in, 16)

                def body(i, s, ip, last):
                    for e in range(NSTEP):
                        if e == 0:
                            pe.wait_ge(d1_in, 16 * i + 16)
                        if e == FIRST:
                            pe.wait_ge(d0_in, 16 * i + 16)
                        slot0_free(i, e, last)
                        second(i, s, e, 0)
                        for h in range(3 * e, 3 * e + 3):
                            if h == 3 * e + 1:
                                if e > 0:
                                    pe.wait_ge(exp_done, 2 * NSTEP * i + 2 * e)
                                second(i, s, e, 1)
                            if h == 3 * e + 2 and e > 0:
                                pv(i, s, e - 1)
                            for half in (0, 1):
                                if not last and (EARLY[LATER_KEYS], EARLY[0])[half] in plan[h]:
                                    pe.wait_ge(stk_in[1 - s][half], LOADS[half] * (ip + 1 + s))
                            ring(i, s, plan[h], last)
                        if e == NSTEP - 1:
                            ring(i, s, tail[:BEFORE], last)
                        if e == D1_AT and not last:
                            pe.wait_ge(exp_done, 2 * NSTEP * i + 2 * e + 1)
                            trans_d(2 * i + 2, pair[0][:, 0, :], s_full[0])
                    pv(i, s, NSTEP - 1)
                    ring(i, s, tail[BEFORE:], last)
                groups(pe, body)

        def w_cols(n, it):
            rows = w_f[:, n * KT * INNER:(n + 1) * KT * INNER].rearrange("p (k c) -> p k c", k=KT)
            return rows[:, :, it * P:(it + 1) * P]

        def w_down(it):
            return w_f[:, 2 * KT * INNER + it * D:2 * KT * INNER + (it + 1) * D]

        o_in, o_tr, o_hi, o_lo, s_proj, s_cp = sem("o_in"), sem("o_tr"), sem("o_hi"), sem("o_lo"), sem("s_proj"), sem("s_cp")
        xc_tr, xc_h, xc_l = sem("xc_tr"), sem("xc_h"), sem("xc_l")
        wg_hi, wg_lo, wd_hi, wd_lo = sem("wg_hi"), sem("wg_lo"), sem("wd_hi"), sem("wd_lo")
        gu_done, silu_done, h_mul, hh_done, hl_done, down_done = (
            sem("gu_done"), sem("silu_done"), sem("h_mul"), sem("hh_done"), sem("hl_done"), sem("down_done"))
        y_sum, y_silu, y_mul, y_add = sem("y_sum"), sem("y_silu"), sem("y_mul"), sem("y_add")
        o_stored = [sem(f"o_stored{n}") for n in range(4)]
        y = bank
        NB = TOK // 512
        C_P, C_OTR, C_YS, C_HL, C_ST = 4, 1, 4, 2, 16

        def blocks(eng, body):
            with eng.Fori(0, NB - 1) as b:
                body(b, False)
            body(NB - 1, True)

        with nc.Block() as block:
            @block.sync
            def _(sp):
                def slot_used(b, u):
                    sp.wait_ge(xuse_p, 4 * b + u + 1)
                    sp.wait_ge(xuse_d, 4 * b + u + 1)

                def body(b, last):
                    for u in range(4):
                        slot_used(b, u)
                        load_x(sp, b if last else b + 1, u)
                    if not last:
                        for u in range(4):
                            sp.wait_ge(xuse_d, 4 * b + u + 5)
                            load_x(sp, b, u)
                    for u in range(4):
                        if last:
                            sp.wait_ge(*((y_add, u // 2 + 1) if u % 2 else (xuse_p, C_P + 4 * b + u // 2 + 1)))
                        else:
                            sp.wait_ge(xuse_p, C_P + 4 * b + u + 1)
                        sp.dma_start(out_t[4 * b + u], s_sb[:, u, :]).then_inc(o_stored[u], 16)
                blocks(sp, body)
                for n in range(4):
                    sp.wait_ge(o_stored[n], C_ST + 4 * TILES)

            @block.gpsimd
            def _(pool):
                for s_, n in ((xuse_p, C_P), (o_tr, C_OTR), (y_silu, C_YS), (hl_done, C_HL),
                              *((o_stored[n], C_ST) for n in range(4))):
                    pool.sem_inc(s_, n)

                def low(dst, src, hi):
                    return pool.tensor_tensor(dst, src, hi.bitcast(F32), ALU.subtract)

                def w_gu(b, it):
                    s = it % 2
                    pool.wait_ge(wg_hi, IT * b + it + 1)
                    for n in range(2):
                        mm = low(ws_lo[s][:, n, :].rearrange("p (k c) -> p k c", k=KT), w_cols(n, it),
                                 ws_hi[s][:, n, :].rearrange("p (k c) -> p k c", k=KT))
                    mm.then_inc(wg_lo, 1)

                def w_d(b, it):
                    s = it % 2
                    pool.wait_ge(wd_hi, IT * b + it + 1)
                    low(ws_lo[s][:, 2, :], w_down(it), ws_hi[s][:, 2, :]).then_inc(wd_lo, 1)

                w_gu(0, 0)
                w_gu(0, 1)
                w_d(0, 0)

                def body(b, last):
                    for it in range(IT):
                        if it + 2 < IT:
                            w_gu(b, it + 2)
                        elif not last:
                            w_gu(b + 1, it + 2 - IT)
                        if it + 1 < IT:
                            w_d(b, it + 1)
                        elif not last:
                            w_d(b + 1, 0)
                    for u in range(4):
                        if last and u % 2:
                            continue
                        pool.wait_ge(y_mul, 4 * b + u + 1)
                        pool.wait_ge(xc_in[u], 32 * b + (32 if last else 48))
                        pool.tensor_tensor(s_sb[:, u, :], s_sb[:, u, :], xin_c[:, u, :], ALU.add).then_inc(xuse_p, 1)
                blocks(pool, body)

            @block.scalar
            def _(act):
                def copy(dst, src):
                    return act.activation(dst, src, ACT.Copy)

                def load_o(b, u):
                    act.wait_ge(o_tr, 4 * b + u + 1)
                    t = 4 * b + u
                    src = o_sb[:, bass.ds((t // QT) * GROUPS, GROUPS), bass.ds(t % QT, 1), :]
                    copy(oin[:, :].rearrange("p (g a w) -> p g a w", g=GROUPS, a=1), src).then_inc(o_in, 1)

                def hi_o(b, u):
                    act.wait_ge(o_tr, C_OTR + 4 * b + u + 1)
                    copy(h_hi[u % 2][:, :], pair[1][:, u % 2, :]).then_inc(o_hi, 1)

                def hi_x(b, u):
                    act.wait_ge(xc_tr, 4 * b + u + 1)
                    copy(xc_hi[:, :, u * P:(u + 1) * P], pair[u // 2][:, u % 2, :].rearrange("p (k c) -> p k c", k=KT)).then_inc(xc_h, 1)

                def copy_s(b, u):
                    act.wait_ge(s_proj, 4 * b + u + 1)
                    act.wait_ge(o_stored[u], 16 * b + 16)
                    copy(s_sb[:, u, :], y[u][:, :]).then_inc(s_cp, 1)

                def w_gu(b, it):
                    for n in range(2):
                        mm = copy(ws_hi[it % 2][:, n, :].rearrange("p (k c) -> p k c", k=KT), w_cols(n, it))
                    mm.then_inc(wg_hi, 1)

                def w_d(b, it):
                    if it > 1 or (it == 0 and not isinstance(b, int)):
                        act.wait_ge(down_done, IT * b + it - 1)
                    copy(ws_hi[it % 2][:, 2, :], w_down(it)).then_inc(wd_hi, 1)

                w_gu(0, 0)
                for u in range(4):
                    hi_x(0, u)
                load_o(0, 0)
                w_gu(0, 1)
                w_d(0, 0)

                def body(b, last):
                    load_o(b, 1)
                    hi_o(b, 0)
                    load_o(b, 2)
                    hi_o(b, 1)
                    copy_s(b, 0)
                    load_o(b, 3)
                    hi_o(b, 2)
                    copy_s(b, 1)
                    hi_o(b, 3)
                    copy_s(b, 2)
                    copy_s(b, 3)
                    for it in range(IT):
                        act.wait_ge(gu_done, IT * b + it + 1)
                        act.wait_ge(hl_done, IT * b + it + 1)
                        act.activation(sg[it % 2][:, :], pair[it % 2][:, 0, :], ACT.Silu).then_inc(silu_done, 1)
                        if it + 2 < IT:
                            w_gu(b, it + 2)
                        elif it + 2 == IT and not last:
                            w_gu(b + 1, 0)
                        act.wait_ge(h_mul, IT * b + it + 1)
                        if it > 1:
                            act.wait_ge(down_done, IT * b + it - 1)
                        copy(h_hi[it % 2][:, :], sg[it % 2][:, :]).then_inc(hh_done, 1)
                        if it + 1 < IT:
                            w_d(b, it + 1)
                        elif not last:
                            for u in range(4):
                                hi_x(b + 1, u)
                            load_o(b + 1, 0)
                            w_gu(b + 1, 1)
                            w_d(b + 1, 0)
                    for u in range(4):
                        if u < 3:
                            act.wait_ge(y_sum, 3 * b + u + 1)
                        else:
                            act.wait_ge(down_done, IT * b + IT)
                        if u > 1:
                            act.wait_ge(y_mul, 4 * b + u - 1)
                        act.activation(sg[u % 2][:, :], y[u][:, :], ACT.Silu).then_inc(y_silu, 1)
                blocks(act, body)

            @block.vector
            def _(dve):
                def norm(b, u, loaded):
                    t = 4 * b + u
                    dve.wait_ge(xc_in[u], loaded)
                    if u > 1:
                        dve.wait_ge(xc_tr, 4 * b + u - 1)
                    dve.tensor_scalar(xnc[:, u % 2, :], xin_c[:, u, :], xmean[:, bass.ds(t, 1)], xrstd[:, bass.ds(t, 1)],
                                      ALU.subtract, ALU.mult).then_inc(xuse_d, 1)

                def lo_o(b, u):
                    dve.wait_ge(o_hi, 4 * b + u + 1)
                    dve.tensor_tensor(h_lo[u % 2][:, :], pair[1][:, u % 2, :], h_hi[u % 2][:, :].bitcast(F32), ALU.subtract)\
                       .then_inc(o_lo, 1)

                def lo_x(b, u):
                    dve.wait_ge(xc_h, 4 * b + u + 1)
                    cols = slice(u * P, (u + 1) * P)
                    dve.tensor_tensor(xc_lo[:, :, cols], pair[u // 2][:, u % 2, :].rearrange("p (k c) -> p k c", k=KT),
                                      xc_hi[:, :, cols].bitcast(F32), ALU.subtract).then_inc(xc_l, 1)

                for u in range(4):
                    norm(0, u, 16)
                for u in range(4):
                    lo_x(0, u)

                def body(b, last):
                    for u in range(4):
                        lo_o(b, u)
                    for it in range(IT):
                        s = it % 2
                        dve.wait_ge(silu_done, IT * b + it + 1)
                        dve.tensor_tensor(sg[s][:, :], pair[s][:, 1, :], sg[s][:, :], ALU.mult).then_inc(h_mul, 1)
                        dve.wait_ge(hh_done, IT * b + it + 1)
                        dve.tensor_tensor(h_lo[s][:, :], sg[s][:, :], h_hi[s][:, :].bitcast(F32), ALU.subtract).then_inc(hl_done, 1)
                        if it >= IT - 2 and not last:
                            for u in range(2 * (it - IT + 2), 2 * (it - IT + 3)):
                                norm(b + 1, u, 32 * b + 32)
                    if not last:
                        for u in range(4):
                            lo_x(b + 1, u)
                    for u in range(4):
                        dve.wait_ge(y_silu, C_YS + 4 * b + u + 1)
                        dve.tensor_tensor(s_sb[:, u, :], sg[u % 2][:, :], s_sb[:, u, :], ALU.mult).then_inc(y_mul, 1)
                        if last and u % 2:
                            dve.wait_ge(y_mul, 4 * b + u + 1)
                            dve.wait_ge(xc_in[u], 32 * b + 32)
                            dve.tensor_tensor(s_sb[:, u, :], s_sb[:, u, :], xin_c[:, u, :], ALU.add).then_inc(y_add, 1)
                blocks(dve, body)

            @block.tensor
            def _(pe):
                def trans_o(b, u):
                    if u == 0:
                        pe.wait_ge(xc_l, 4 * b + 4)
                    pe.wait_ge(o_in, 4 * b + u + 1)
                    if u > 1:
                        pe.wait_ge(o_lo, 4 * b + u - 1)
                    for k in range(KT):
                        mm = pe.transpose(pair[1][:, u % 2, k * P:(k + 1) * P], oin[:, k * P:(k + 1) * P], ident[:, :])
                    mm.then_inc(o_tr, 1)

                def trans_x(b, u):
                    pe.wait_ge(xuse_d, 4 * b + u + 1)
                    if not isinstance(b, int) and u % 2 == 0:
                        pe.wait_ge(h_mul, IT * b - 1 + u // 2)
                    for k in range(KT):
                        mm = pe.transpose(pair[u // 2][:, u % 2, k * P:(k + 1) * P], xnc[:, u % 2, k * P:(k + 1) * P], ident[:, :])
                    mm.then_inc(xc_tr, 1)

                def terms(l_hi, l_lo, r_hi, r_lo):
                    return (l_lo, r_hi), (l_hi, r_lo), (l_hi, r_hi)

                def s_project(b, u):
                    pe.wait_ge(o_lo, 4 * b + u + 1)
                    pe.wait_ge(y_silu, 4 * b + u + 1)
                    for k in range(KT):
                        cols = slice(k * P, (k + 1) * P)
                        for n, (l, r) in enumerate(terms(h_hi[u % 2][:, cols], h_lo[u % 2][:, cols], wo_hi[:, k, :], wo_lo[:, k, :])):
                            mm = pe.matmul(y[u][:, :], l, r, start=(k == 0 and n == 0), stop=(k == KT - 1 and n == 2))
                    mm.then_inc(s_proj, 1)

                def gate_up(b, it):
                    s = it % 2
                    pe.wait_ge(wg_lo, IT * b + it + 1)
                    if it == 1:
                        pe.wait_ge(o_lo, 4 * b + 4)
                    elif it > 1:
                        pe.wait_ge(h_mul, IT * b + it - 1)
                    for g in range(2):
                        for k in range(KT):
                            cols = slice(k * P, (k + 1) * P)
                            for n, (l, r) in enumerate(terms(ws_hi[s][:, g, cols], ws_lo[s][:, g, cols], xc_hi[:, k, :], xc_lo[:, k, :])):
                                mm = pe.matmul(pair[s][:, g, :], l, r, start=(k == 0 and n == 0), stop=(k == KT - 1 and n == 2))
                    mm.then_inc(gu_done, 1)

                def down(b, it):
                    s = it % 2
                    if it == 0:
                        pe.wait_ge(s_cp, 4 * b + 4)
                    pe.wait_ge(wd_lo, IT * b + it + 1)
                    pe.wait_ge(hl_done, C_HL + IT * b + it + 1)
                    for t in range(4):
                        cols = slice(t * P, (t + 1) * P)
                        for n, (l, r) in enumerate(terms(h_hi[s][:, cols], h_lo[s][:, cols], ws_hi[s][:, 2, :], ws_lo[s][:, 2, :])):
                            mm = pe.matmul(y[t][:, :], l, r, start=(it == 0 and n == 0), stop=(it == IT - 1 and n == 2))
                        if it == IT - 1 and t < 3:
                            mm.then_inc(y_sum, 1)
                    mm.then_inc(down_done, 1)

                for u in range(4):
                    trans_x(0, u)

                def body(b, last):
                    trans_o(b, 0)
                    gate_up(b, 0)
                    trans_o(b, 1)
                    s_project(b, 0)
                    trans_o(b, 2)
                    s_project(b, 1)
                    trans_o(b, 3)
                    s_project(b, 2)
                    s_project(b, 3)
                    for it in range(IT):
                        if it + 1 < IT:
                            gate_up(b, it + 1)
                        elif not last:
                            for u in range(4):
                                trans_x(b + 1, u)
                        down(b, it)
                blocks(pe, body)


def _constants():
    import numpy as np

    def bits(a):
        return (np.ascontiguousarray(a, np.float32).view(np.uint32) >> 16).astype(np.uint16)

    def bf(a):
        u = np.ascontiguousarray(a, np.float32).view(np.uint32).astype(np.uint64)
        return ((u + 0x7FFF + ((u >> 16) & 1)) & 0xFFFF0000).astype(np.uint32).view(np.float32)
    eye = np.eye(P, dtype=np.float32)
    tri = np.zeros((P, 512), np.float32)
    tri[:, 512 - P:] = np.where(np.arange(P)[None, :] <= np.arange(P)[:, None], 0.0, -1e30)
    behind = np.where(np.arange(P)[:, None] > np.arange(P)[None, :], -1e30, 0.0).astype(np.float32)
    m = np.arange(1, HEADS + 1, dtype=np.float32) * (8.0 / HEADS)
    slope = ((1.0 / np.power(2.0, m)) / SCALE).astype(np.float32)
    h = bf(slope)
    mid = bf(slope - h)
    low = bf(slope - h - mid)
    pos = np.arange(SEQ)
    far, near, one = (pos // P * P).astype(np.float32), (pos % P).astype(np.float32), np.ones(SEQ, np.float32)
    q = np.zeros((HEADS, 12, SEQ), np.float32)
    k = np.zeros((HEADS, 15, SEQ), np.float32)
    for n in range(HEADS):
        for i, part in enumerate((h[n], mid[n], low[n])):
            q[n, 4 * i:4 * i + 4] = part * one, -far, part * one, -near
            k[n, 4 * i:4 * i + 4] = far, part * one, near, part * one
        k[n, 12:] = 1.0

    q = q.reshape(GROUPS, GH, 12, SEQ).transpose(0, 2, 1, 3)
    k = k.reshape(GROUPS, GH, 15, SEQ).transpose(0, 2, 1, 3)
    return {"ident": eye, "identb": bits(eye), "tri": tri, "behind": bits(behind), "qrows": bits(q), "krows": bits(k)}


def kernel(L0_attn_hidden_states, L0_attn_Wqkv, L0_attn_q_ln_w, L0_attn_q_ln_b, L0_attn_k_ln_w, L0_attn_k_ln_b,
           L0_attn_Wout, L0_ffn_gate_w, L0_ffn_gate_z, L0_ffn_gate_s, L0_ffn_up_w, L0_ffn_up_z, L0_ffn_up_s,
           L0_ffn_down_w, L0_ffn_down_z, L0_ffn_down_s):
    import numpy as np
    import concourse.bacc as bacc
    from concourse.bass_utils import run_bass_kernel_spmd as run

    A = np.asarray

    def packed(gate, up, down, rows):
        d = A(down).reshape(IT, rows, D).transpose(1, 0, 2).reshape(rows, KT, INNER).transpose(1, 0, 2)
        return np.ascontiguousarray(np.concatenate([A(gate).reshape(KT, rows, INNER), A(up).reshape(KT, rows, INNER), d]))
    wproj = np.concatenate([A(L0_attn_Wqkv).T, A(L0_attn_Wout).T], axis=1).reshape(KT, P, 4 * D)
    arrays = {
        "x": A(L0_attn_hidden_states),
        "wproj": np.ascontiguousarray(wproj),
        "lnw": np.stack([A(L0_attn_q_ln_w), A(L0_attn_q_ln_b), A(L0_attn_k_ln_w), A(L0_attn_k_ln_b)]),
        "w_all": packed(L0_ffn_gate_w, L0_ffn_up_w, L0_ffn_down_w, P).reshape(JOBS, P, 2, HALF)
        .transpose(0, 2, 1, 3).reshape(NHALF, P, HALF),
        "z_all": packed(L0_ffn_gate_z, L0_ffn_up_z, L0_ffn_down_z, 1).reshape(NHALF, HALF),
        "s_all": packed(L0_ffn_gate_s, L0_ffn_up_s, L0_ffn_down_s, 1).reshape(NHALF, HALF),
        **_constants(),
    }
    nc = bacc.Bacc("TRN2", target_bir_lowering=False, num_devices=1)
    aps = {}
    for name, a in arrays.items():
        dt = BF16 if a.dtype == np.uint16 else mybir.dt.from_np(a.dtype)
        if a.dtype == np.uint16:
            aps[name] = nc.dram_tensor(f"in_{name}", a.shape, mybir.dt.from_np(a.dtype), kind="ExternalInput").ap().bitcast(BF16)
        else:
            aps[name] = nc.dram_tensor(f"in_{name}", a.shape, dt, kind="ExternalInput").ap()
    out = nc.dram_tensor("out", (BATCH, SEQ, D), F32, kind="ExternalOutput").ap()
    build(nc, aps["x"], aps["wproj"], aps["lnw"], aps["w_all"], aps["z_all"], aps["s_all"], aps["ident"],
          aps["identb"], aps["tri"], aps["behind"], aps["qrows"], aps["krows"], out)
    r = run(nc, [{f"in_{n}": a for n, a in arrays.items()}], core_ids=[0])
    return r.results[0]["out"]
```
